# Optimizing a Trainium2 kernel written in Bass

```python
import numpy as np
import jax
import jax.numpy as jnp

def _softmax(x, axis=-1):
    return jax.nn.softmax(x, axis=axis)

def _gelu(x):
    return jax.nn.gelu(x, approximate=True)

def _silu(x):
    return jax.nn.silu(x)

def _sigmoid(x):
    return jax.nn.sigmoid(x)

def _layernorm(x, axis=-1, eps=1e-05):
    m = jnp.mean(x, axis=axis, keepdims=True)
    v = jnp.var(x, axis=axis, keepdims=True)
    return (x - m) / jnp.sqrt(v + eps)

def _scatter_add(tgt, idx, src, axis=0):
    return tgt.at[idx].add(src)

def _segment_sum(src, seg, n):
    return jax.ops.segment_sum(src, seg, n)
kernel_name = 'mk_early_fusion_d1_tok_img768_r4_0e612b'

def setup_inputs(seed: int=0):
    np.random.seed(seed)
    _w = jnp.asarray

    def _rec_inputs():
        import jax
        import jax.numpy as jnp
        _rk = jax.random.key(seed)
        x = -0.000222058 + 0.999998 * jax.random.normal(jax.random.fold_in(_rk, 1), (32, 3, 224, 224), jnp.float32)
        txt = -5.78238e-05 + 0.554219 * jax.random.normal(jax.random.fold_in(_rk, 2), (32, 77, 192), jnp.float32)
        return (x, txt)
    x, txt = _rec_inputs()

    def _L0_tok_setup():
        import jax, jax.numpy as jnp
        import numpy as np
        from jax import lax
        N_BITS = 4
        PATCH = 16

        def _hilbert_points(p):
            n = 1 << p
            pts = np.zeros((n * n, 2), dtype=np.int32)
            for d in range(n * n):
                t, x, y, s = (d, 0, 0, 1)
                while s < n:
                    rx = 1 & t // 2
                    ry = 1 & (t ^ rx)
                    if ry == 0:
                        if rx == 1:
                            x = s - 1 - x
                            y = s - 1 - y
                        x, y = (y, x)
                    x += s * rx
                    y += s * ry
                    t //= 4
                    s *= 2
                pts[d, 0] = x
                pts[d, 1] = y
            return pts
        _INDEX_MAP = _hilbert_points(N_BITS)
        key = jax.random.key(seed)
        k1, k2 = jax.random.split(key)
        x = jax.random.normal(k1, (128, 3, 64, 64), dtype=jnp.float32)
        W = jax.random.normal(k2, (192, 3, PATCH, PATCH), dtype=jnp.float32) * 0.02
        b = jnp.zeros((192,), dtype=jnp.float32)
        return {'x': x, 'W': W, 'b': b}
    _L0_tok_all = _L0_tok_setup()
    _L0_tok_in = {k: v for k, v in _L0_tok_all.items() if k in ('W', 'b')}
    del _L0_tok_all

    def _L0_attn_setup():
        import jax, jax.numpy as jnp
        import numpy as np
        B, L, D = (4, 512, 192)
        H, K = (12, 9)
        IPG = D // H
        PAD = (K - 1) // 2

        def _sdconv(query, dw_w, pw_w, pw_b, ak_w, ak_b, pt_w, pt_b):
            b, l, d = query.shape
            x = query.transpose(0, 2, 1)
            dw = jax.lax.conv_general_dilated(x, dw_w, window_strides=(1,), padding=[(PAD, PAD)], feature_group_count=d, dimension_numbers=('NCH', 'OIH', 'NCH'))
            dwg = dw.reshape(b, H, IPG, l)
            pw = jnp.einsum('bhil,hoi->bhol', dwg, pw_w).reshape(b, d, l) + pw_b[None, :, None]
            key_conv_attn = pw.transpose(0, 2, 1)
            conv_attn = key_conv_attn * query
            ca = conv_attn.reshape(b, l, H, IPG)
            kern = jnp.einsum('blhi,hki->blhk', ca, ak_w) + ak_b.reshape(H, K)
            w = jax.nn.softmax(kern, axis=-1)
            v = query @ pt_w.T + pt_b
            vp = jnp.pad(v, ((0, 0), (PAD, PAD), (0, 0)))
            idx = jnp.arange(l)[:, None] + jnp.arange(K)[None, :]
            win = vp[:, idx]
            winh = win.reshape(b, l, K, H, IPG)
            out = jnp.einsum('blkhd,blhk->blhd', winh, w).reshape(b, l, d)
            return out
        key = jax.random.key(seed)
        ks = jax.random.split(key, 8)
        s = lambda k, shape, scale: jax.random.normal(k, shape, dtype=jnp.float32) * scale
        return {'query': s(ks[0], (B, L, D), 1.0), 'dw_w': s(ks[1], (D, 1, K), 0.1), 'pw_w': s(ks[2], (H, IPG, IPG), 0.05), 'pw_b': s(ks[3], (D,), 0.02), 'ak_w': s(ks[4], (H, K, IPG), 0.05), 'ak_b': s(ks[5], (H * K,), 0.02), 'pt_w': s(ks[6], (D, D), 0.02), 'pt_b': s(ks[7], (D,), 0.02)}
    _L0_attn_all = _L0_attn_setup()
    _L0_attn_in = {k: v for k, v in _L0_attn_all.items() if k in ('dw_w', 'pw_w', 'pw_b', 'ak_w', 'ak_b', 'pt_w', 'pt_b')}
    del _L0_attn_all

    def _L0_ffn_setup():
        import jax, jax.numpy as jnp
        import numpy as np
        E = 8
        TOP_K = 2
        CAP_RATIO = 1.2
        key = jax.random.key(seed)
        k1, k2, k3, k4 = jax.random.split(key, 4)
        B, L, D, H = (2, 512, 192, 512)
        x = jax.random.normal(k1, (B, L, D), dtype=jnp.float32)
        Wg = jax.random.normal(k2, (D, E), dtype=jnp.float32) * 0.02
        W1 = jax.random.normal(k3, (E, D, 2 * H), dtype=jnp.float32) * 0.02
        W2 = jax.random.normal(k4, (E, H, D), dtype=jnp.float32) * 0.02
        return {'x': x, 'Wg': Wg, 'W1': W1, 'W2': W2}
    _L0_ffn_all = _L0_ffn_setup()
    _L0_ffn_in = {k: v for k, v in _L0_ffn_all.items() if k in ('Wg', 'W1', 'W2')}
    del _L0_ffn_all
    return {'x': x, 'txt': txt, 'L0_tok_W': _L0_tok_in['W'], 'L0_tok_b': _L0_tok_in['b'], 'L0_attn_dw_w': _L0_attn_in['dw_w'], 'L0_attn_pw_w': _L0_attn_in['pw_w'], 'L0_attn_pw_b': _L0_attn_in['pw_b'], 'L0_attn_ak_w': _L0_attn_in['ak_w'], 'L0_attn_ak_b': _L0_attn_in['ak_b'], 'L0_attn_pt_w': _L0_attn_in['pt_w'], 'L0_attn_pt_b': _L0_attn_in['pt_b'], 'L0_ffn_Wg': _L0_ffn_in['Wg'], 'L0_ffn_W1': _L0_ffn_in['W1'], 'L0_ffn_W2': _L0_ffn_in['W2']}

def reference(x, txt, L0_tok_W, L0_tok_b, L0_attn_dw_w, L0_attn_pw_w, L0_attn_pw_b, L0_attn_ak_w, L0_attn_ak_b, L0_attn_pt_w, L0_attn_pt_b, L0_ffn_Wg, L0_ffn_W1, L0_ffn_W2):
    import jax
    import jax.numpy as jnp

    def _L0_tok_ref(x, W, b):
        import jax, jax.numpy as jnp
        import numpy as np
        from jax import lax
        N_BITS = 4
        PATCH = 16

        def _hilbert_points(p):
            n = 1 << p
            pts = np.zeros((n * n, 2), dtype=np.int32)
            for d in range(n * n):
                t, x, y, s = (d, 0, 0, 1)
                while s < n:
                    rx = 1 & t // 2
                    ry = 1 & (t ^ rx)
                    if ry == 0:
                        if rx == 1:
                            x = s - 1 - x
                            y = s - 1 - y
                        x, y = (y, x)
                    x += s * rx
                    y += s * ry
                    t //= 4
                    s *= 2
                pts[d, 0] = x
                pts[d, 1] = y
            return pts
        _INDEX_MAP = _hilbert_points(N_BITS)
        y = lax.conv_general_dilated(x, W, window_strides=(PATCH, PATCH), padding='VALID', dimension_numbers=('NCHW', 'OIHW', 'NCHW'))
        y = y + b[None, :, None, None]
        ix = jnp.asarray(_INDEX_MAP[:, 0])
        iy = jnp.asarray(_INDEX_MAP[:, 1])
        flat = y[:, :, ix, iy]
        return jnp.transpose(flat, (0, 2, 1))

    def _L0_attn_ref(query, dw_w, pw_w, pw_b, ak_w, ak_b, pt_w, pt_b):
        import jax, jax.numpy as jnp
        import numpy as np
        B, L, D = (4, 512, 192)
        H, K = (12, 9)
        IPG = D // H
        PAD = (K - 1) // 2

        def _sdconv(query, dw_w, pw_w, pw_b, ak_w, ak_b, pt_w, pt_b):
            b, l, d = query.shape
            x = query.transpose(0, 2, 1)
            dw = jax.lax.conv_general_dilated(x, dw_w, window_strides=(1,), padding=[(PAD, PAD)], feature_group_count=d, dimension_numbers=('NCH', 'OIH', 'NCH'))
            dwg = dw.reshape(b, H, IPG, l)
            pw = jnp.einsum('bhil,hoi->bhol', dwg, pw_w).reshape(b, d, l) + pw_b[None, :, None]
            key_conv_attn = pw.transpose(0, 2, 1)
            conv_attn = key_conv_attn * query
            ca = conv_attn.reshape(b, l, H, IPG)
            kern = jnp.einsum('blhi,hki->blhk', ca, ak_w) + ak_b.reshape(H, K)
            w = jax.nn.softmax(kern, axis=-1)
            v = query @ pt_w.T + pt_b
            vp = jnp.pad(v, ((0, 0), (PAD, PAD), (0, 0)))
            idx = jnp.arange(l)[:, None] + jnp.arange(K)[None, :]
            win = vp[:, idx]
            winh = win.reshape(b, l, K, H, IPG)
            out = jnp.einsum('blkhd,blhk->blhd', winh, w).reshape(b, l, d)
            return out
        return _sdconv(query, dw_w, pw_w, pw_b, ak_w, ak_b, pt_w, pt_b)

    def _L0_ffn_ref(x, Wg, W1, W2):
        import jax, jax.numpy as jnp
        import numpy as np
        E = 8
        TOP_K = 2
        CAP_RATIO = 1.2
        B, L, D = x.shape
        H = W2.shape[1]
        xf = x.reshape(-1, D)
        N = xf.shape[0]
        capacity = int(CAP_RATIO * N / E)
        logits = xf @ Wg
        scores, idx = jax.lax.top_k(logits, TOP_K)
        weights = jax.nn.softmax(scores, axis=-1)
        xpad = jnp.concatenate([xf, jnp.zeros((1, D), xf.dtype)], axis=0)
        wpad_zero = jnp.zeros((1,), weights.dtype)
        out = jnp.zeros((N, D), x.dtype)
        for k in range(TOP_K):
            ik = idx[:, k]
            onehot = ik[:, None] == jnp.arange(E)[None, :]
            pos = jnp.cumsum(onehot, axis=0) - 1
            posk = jnp.take_along_axis(pos, ik[:, None], axis=1)[:, 0]
            keep = posk < capacity
            buf = jnp.full((E, capacity), N, dtype=jnp.int32)
            buf = buf.at[ik, posk].set(jnp.arange(N, dtype=jnp.int32), mode='drop')
            xg = xpad[buf]
            h = jnp.einsum('ecd,edh->ech', xg, W1)
            act = h[..., :H] * jax.nn.silu(h[..., H:])
            ye = jnp.einsum('ech,ehd->ecd', act, W2)
            wk = jnp.where(keep, weights[:, k], 0.0)
            w_buf = jnp.concatenate([wk, wpad_zero])[buf]
            out = out.at[buf.reshape(-1)].add((w_buf[..., None] * ye).reshape(E * capacity, D), mode='drop')
        return out.reshape(B, L, D)
    h = _L0_tok_ref(x, L0_tok_W, L0_tok_b)
    h = jnp.concatenate([h, txt], axis=1)
    h = h + _L0_attn_ref(_layernorm(h, axis=-1), L0_attn_dw_w, L0_attn_pw_w, L0_attn_pw_b, L0_attn_ak_w, L0_attn_ak_b, L0_attn_pt_w, L0_attn_pt_b)
    h = h + _L0_ffn_ref(_layernorm(h, axis=-1), L0_ffn_Wg, L0_ffn_W1, L0_ffn_W2)
    return h

_drawn_inputs = setup_inputs


def setup_inputs(seed=0):
    import zlib

    import numpy as np

    out = dict(_drawn_inputs(seed))
    spreads = {'L0_tok_b': (0.0, 0.1)}
    factors = {'L0_attn_dw_w': 8.0,
     'L0_attn_pw_w': 8.0,
     'L0_attn_pw_b': 8.0,
     'L0_attn_ak_w': 8.0,
     'L0_attn_ak_b': 8.0,
     'L0_ffn_Wg': 8.831}
    for name, (base, spread) in spreads.items():
        noise = np.random.default_rng([zlib.crc32(name.encode()), seed]).standard_normal(out[name].shape)
        drawn = base * np.exp(spread * noise) if base else spread * noise
        out[name] = jnp.asarray(drawn.astype(out[name].dtype))
    for name, factor in factors.items():
        out[name] = (out[name] * factor).astype(out[name].dtype)
    return out
```

```python
import numpy as np
import concourse.bass as bass
from concourse import mybir
from contextlib import ExitStack

B, CIN, IMG, PATCH = 32, 3, 224, 16
GRID = IMG // PATCH
CURVE = 16
TI, TT, D = CURVE * CURVE, 77, 192
L = TI + TT
KC = CIN * PATCH * PATCH // 128
H, IPG, K = 12, 16, 9
PAD = (K - 1) // 2
D2 = D - 128
HA = 128 // IPG
HB = H - HA
E, TOPK, HID = 8, 2, 512
CAP = int(1.2 * B * L / E)
SLOT_TILE, CHUNK = 400, 100
TPE = -(-TOPK * CAP // SLOT_TILE)
CAPE = TPE * SLOT_TILE
NS = E * CAPE
EPS = 1e-5

NPAIR = B // 2
CT = [128, 128, TT]
ROW = 2 * D + H * K
SEG, R = 16, 21
LROWS = SEG * R + 2 * PAD
GIMG = 128 // SEG
NG = B // GIMG
RL = L - (SEG - 1) * R
SL = 7
NSL = R // SL
BIG = 1e30


def build(nc, x, txt, wpatch, tokb, dw, pw, pwb, akA, akB, akb, ptA, ptB, ptb, wg, W1, W2,
          ident, lower, revrank, valid, slotbase, out):
    fp32, i32 = mybir.dt.float32, mybir.dt.int32
    ALU, ACT, AX = mybir.AluOpType, mybir.ActivationFunctionType, mybir.AxisListType

    rows = nc.dram_tensor("token_rows", (B, LROWS, ROW), fp32, kind="Internal").ap()
    xslots = nc.dram_tensor("expert_inputs", (NS, D), fp32, kind="Internal").ap()
    yslots = nc.dram_tensor("expert_outputs", (NS + 1, D), fp32, kind="Internal").ap()

    def wait(eng, sem, value):
        if isinstance(value, int) and value <= 0:
            return
        eng.wait_ge(sem, value)

    def settled(eng):
        eng.sem_inc(passed, 1)

    top = ExitStack()
    with top:
        def allocator(stack):
            return (lambda n, s, dt=fp32: stack.enter_context(nc.sbuf_tensor(n, s, dt)),
                    lambda n: stack.enter_context(nc.psum_tensor(n, [128, 512], fp32)),
                    lambda n: stack.enter_context(nc.semaphore(n)))
        sb, _, sem = allocator(top)

        idn = sb("identity", [128, 128])
        hpost = sb("hidden", [128, NG * R, D])
        idx_all = sb("slot_of_token", [128, NG, TOPK, R], i32)
        wk_all = sb("weight_of_token", [128, NG, TOPK, R])
        const_loaded = sem("const_loaded")
        passed = sem("passed")

        st = ExitStack()
        with st:
            sb, pb, sem = allocator(st)
            wp_sb = sb("wp_sb", [128, KC, D])
            tokb_sb = sb("tokb_sb", [128, 2 * D])
            dw_sb = sb("dw_sb", [128, 2, K])
            pw_sb = sb("pw_sb", [128, 2, 128])
            pwb_sb = sb("pwb_sb", [128, 2])
            akA_sb = sb("akA_sb", [128, HA * K])
            akB_sb = sb("akB_sb", [128, 2 * HB * K])
            ptA_sb = sb("ptA_sb", [128, D])
            ptB_sb = sb("ptB_sb", [128, 2 * D])
            ptb_sb = sb("ptb_sb", [128, 2 * D])
            conv_w = sb("conv_w", [128, 2, K, 128])
            xb = [sb(f"patches{u}", [128, 2, KC * TI]) for u in range(2)]
            rowb = [sb(f"rowbuf{u}", [128, 3, 2, ROW]) for u in range(2)]
            qn = [sb(f"normed{u}", [128, 3, 2 * D]) for u in range(2)]
            TILE_AT = [0, 2 * 128, 128]
            qT = [sb(f"normedT{u}", [128, 3, L + 2 * PAD]) for u in range(2)]
            ca = [sb(f"conv_attn{u}", [128, 3, L]) for u in range(2)]
            stats = sb("stats", [128, 6, 6])
            mv = sb("mean_var", [128, 6, 2])
            vare = sb("var_eps", [128, 6])
            rstd = sb("rstd", [128, 6])
            mhalf = sb("minus_half", [128, R])
            zeros = sb("zeros", [128, 4 * ROW])

            bankH = [pb(f"bankH{c}") for c in range(2)]
            bankT = [pb(f"bankT{c}") for c in range(2)]
            bankK = [pb(f"bankK{c}") for c in range(2)]
            bankV, bankN = pb("bankV"), pb("bankN")

            zeroed = sem("zeroed")
            fill_done = sem("fill_done")
            x_loaded = [sem(f"x_loaded{u}") for u in range(2)]
            txt_loaded = [sem(f"txt_loaded{u}") for u in range(2)]
            row_stored = [sem(f"row_stored{u}") for u in range(2)]
            conv_w_ready = sem("conv_w_ready")
            h_ready = sem("h_ready")
            h_in_rows = sem("h_in_rows")
            stats_done = sem("stats_done")
            aggr_done = sem("aggr_done")
            eps_added = sem("eps_added")
            rstd_ready = sem("rstd_ready")
            half_set = sem("half_set")
            qn_ready = sem("qn_ready")
            tq_ready = sem("tq_ready")
            qT_done = sem("qT_done")
            key_ready = sem("key_ready")
            ca_done = sem("ca_done")
            v_ready = sem("v_ready")
            v_evac = sem("v_evac")
            kern_ready = sem("kern_ready")
            kern_evac = sem("kern_evac")

            block = st.enter_context(nc.Block())

            CONSTS = [(idn[:, :], ident), (wp_sb[:, :, :], wpatch), (tokb_sb[:, :], tokb), (dw_sb[:, :, :], dw),
                      (pw_sb[:, :, :], pw), (pwb_sb[:, :], pwb), (akA_sb[:, :], akA), (akB_sb[:, :], akB),
                      (ptA_sb[:, :], ptA), (ptB_sb[:, :], ptB), (ptb_sb[:, :], ptb)]
            NCONST = 16 * len(CONSTS)

            def peeled(eng, body):
                body(0)
                with eng.Fori(1, NPAIR // 2 - 1) as i:
                    body(i)
                body(NPAIR // 2 - 1)

            @block.sync
            def _(sp):
                def load_x(i, u):
                    p = 2 * i + u
                    sp.dma_start(xb[u][:, :, :], x[bass.ds(2 * p, 2), :, :].rearrange("b p f -> p b f"))\
                      .then_inc(x_loaded[u], 16)

                def load_txt(i, u):
                    p = 2 * i + u
                    wait(sp, row_stored[u], 64 * i)
                    sp.dma_start(rowb[u][0:TT, 2, :, D:2 * D],
                                 txt[bass.ds(2 * p, 2), :, :].rearrange("b t d -> t b d")).then_inc(txt_loaded[u], 16)

                def store(i, u):
                    p = 2 * i + u
                    sp.wait_ge(v_evac, 3 * p + 3)
                    sp.wait_ge(kern_evac, 3 * p + 3)
                    for m in range(2):
                        img = rows[bass.ds(2 * p + m, 1), :, :]
                        sp.dma_start(img[:, PAD:PAD + TI, :].rearrange("b (c p) f -> p (b c) f", p=128),
                                     rowb[u][:, 0:2, m, :]).then_inc(row_stored[u], 16)
                        sp.dma_start(img[:, PAD + TI:PAD + L, :].rearrange("b p f -> p (b f)"),
                                     rowb[u][0:TT, 2, m, :]).then_inc(row_stored[u], 16)

                load_x(0, 0)
                for dst, src in CONSTS:
                    sp.dma_start(dst, src).then_inc(const_loaded, 16)
                load_x(0, 1)
                sp.wait_ge(zeroed, 1)
                for u in range(2):
                    load_txt(0, u)

                def body(i):
                    for u in range(2):
                        store(i, u)
                        if not (isinstance(i, int) and i == NPAIR // 2 - 1):
                            sp.wait_ge(h_ready, 2 * (2 * i + u) + 2)
                            load_x(i + 1, u)
                            load_txt(i + 1, u)
                peeled(sp, body)
                for u in range(2):
                    sp.wait_ge(row_stored[u], 64 * (NPAIR // 2))
                sp.wait_ge(fill_done, 16 * (3 + NS * D // 128 // 1920 + 1))

            @block.gpsimd
            def _(pool):
                nc.gpsimd.memset(mhalf[:, :], -0.5).then_inc(half_set, 1)
                pool.wait_ge(half_set, 1)

                def body(i):
                    for u in range(2):
                        p = 2 * i + u
                        pool.wait_ge(aggr_done, p + 1)
                        settled(pool)
                        nc.gpsimd.tensor_scalar(vare[:, :], mv[:, :, 1], EPS, None, ALU.add).then_inc(eps_added, 1)
                        pool.wait_ge(eps_added, p + 1)
                        nc.gpsimd.tensor_tensor(rstd[:, :], vare[:, :], mhalf[:, 0:6], ALU.pow).then_inc(rstd_ready, 1)
                peeled(pool, body)

            @block.scalar
            def _(act):
                act.wait_ge(zeroed, 1)
                z = 4 * ROW
                act.dma_start(rows[:, 0:PAD, :].rearrange("b r f -> b (r f)"), zeros[0:B, 0:z]).then_inc(fill_done, 16)
                tail = LROWS - PAD - L
                act.dma_start(rows[:, PAD + L:PAD + L + 4, :].rearrange("b r f -> b (r f)"),
                              zeros[0:B, 0:z]).then_inc(fill_done, 16)
                act.dma_start(rows[:, PAD + L + 4:LROWS, :].rearrange("b r f -> b (r f)"),
                              zeros[0:B, 0:(tail - 4) * ROW]).then_inc(fill_done, 16)
                xz = xslots.rearrange("(p n f) d -> p n (f d)", p=128, f=10)
                for n in range(NS * D // 128 // 1920):
                    act.dma_start(xz[:, n, :], zeros[:, 0:1920]).then_inc(fill_done, 16)
                act.dma_start(yslots[NS:NS + 1, :], zeros[0:1, 0:D]).then_inc(fill_done, 16)

                def body(i):
                    for u in range(2):
                        p = 2 * i + u
                        for t in range(3):
                            act.wait_ge(tq_ready, 3 * p + t + 1)
                            if t == 0:
                                wait(act, ca_done, 3 * p - 3)
                            nc.scalar.copy(qT[u][:, t, PAD:PAD + L], bankT[(u + t) % 2][:, 0:L]).then_inc(qT_done, 1)
                        for c in range(3):
                            act.wait_ge(kern_ready, 3 * p + c + 1)
                            if c == 0:
                                wait(act, row_stored[u], 64 * i)
                            T = CT[c]
                            nc.scalar.copy(rowb[u][0:T, c, :, 2 * D:2 * D + HA * K],
                                           bankN[0:T, 0:2 * HA * K].rearrange("p (m k) -> p m k", m=2))
                            nc.scalar.copy(rowb[u][0:T, c, :, 2 * D + HA * K:ROW],
                                           bankN[0:T, 2 * HA * K:2 * H * K].rearrange("p (m k) -> p m k", m=2))\
                              .then_inc(kern_evac, 1)
                peeled(act, body)

            @block.vector
            def _(dve):
                for u in range(2):
                    nc.vector.memset(qT[u][:, :, :], 0.0)
                    nc.vector.memset(rowb[u][:, 2, :, D:2 * D], 0.0)
                nc.vector.memset(zeros[:, :], 0.0).then_inc(zeroed, 1)
                dve.wait_ge(const_loaded, NCONST)
                for t in range(2):
                    for k in range(K):
                        last = nc.vector.tensor_scalar(conv_w[:, t, k, :], pw_sb[:, t, :], dw_sb[:, t, k:k + 1],
                                                       None, ALU.mult)
                last.then_inc(conv_w_ready, 1)

                def norm(i, u):
                    p = 2 * i + u
                    wait(dve, row_stored[u], 64 * i)
                    for c in range(2):
                        dve.wait_ge(h_ready, 2 * p + c + 1)
                        nc.vector.tensor_tensor(rowb[u][:, c, :, D:2 * D],
                                                bankH[c][:, 0:2 * D].rearrange("p (m d) -> p m d", m=2),
                                                tokb_sb[:, :].rearrange("p (m d) -> p m d", m=2), ALU.add)\
                          .then_inc(h_in_rows, 1)
                    dve.wait_ge(txt_loaded[u], 16 * (i + 1))
                    dve.wait_ge(h_in_rows, 2 * p + 2)
                    for c in (2, 0, 1):
                        for m in range(2):
                            last = nc.vector.bn_stats(stats[:, 2 * c + m, :], rowb[u][:, c, m, D:2 * D])
                    last.then_inc(stats_done, 1)
                    dve.wait_ge(stats_done, p + 1)
                    settled(dve)
                    for j in range(6):
                        last = nc.vector.bn_aggr(mv[:, j, :], stats[:, j, :])
                    last.then_inc(aggr_done, 1)
                    dve.wait_ge(aggr_done, p + 1)
                    dve.wait_ge(rstd_ready, p + 1)
                    wait(dve, tq_ready, 3 * p - 3)
                    for j in range(6):
                        c, m = j // 2, j % 2
                        parts = [(0, 0, D)] if m == 0 else [(2 * 128, 0, 128), (D, 128, D2)]
                        for to, ch, n in parts:
                            last = nc.vector.tensor_scalar(qn[u][:, c, to:to + n],
                                                           rowb[u][:, c, m, D + ch:D + ch + n],
                                                           mv[:, j, 0:1], rstd[:, j:j + 1], ALU.subtract, ALU.mult)
                    last.then_inc(qn_ready, 1)

                def attend(i, u):
                    p = 2 * i + u
                    for t in range(3):
                        dve.wait_ge(key_ready, 3 * p + t + 1)
                        wait(dve, kern_ready, 3 * p - 3)
                        nc.vector.scalar_tensor_tensor(ca[u][:, t, :], bankK[(u + t) % 2][:, 0:L],
                                                       pwb_sb[:, t // 2:t // 2 + 1], qT[u][:, t, PAD:PAD + L],
                                                       ALU.add, ALU.mult).then_inc(ca_done, 1)
                        c = t
                        T = CT[c]
                        dve.wait_ge(v_ready, 3 * p + c + 1)
                        nc.vector.tensor_tensor(rowb[u][0:T, c, :, 0:D],
                                                bankV[0:T, 0:2 * D].rearrange("p (m d) -> p m d", m=2),
                                                ptb_sb[0:T, :].rearrange("p (m d) -> p m d", m=2), ALU.add)\
                          .then_inc(v_evac, 1)

                norm(0, 0)

                def body(i):
                    norm(i, 1)
                    attend(i, 0)
                    if not (isinstance(i, int) and i == NPAIR // 2 - 1):
                        norm(i + 1, 0)
                    attend(i, 1)
                peeled(dve, body)

            @block.tensor
            def _(pe):
                def patch(i, u):
                    p = 2 * i + u
                    pe.wait_ge(x_loaded[u], 16 * (i + 1))
                    for c in range(2):
                        wait(pe, h_in_rows, 2 * p + c - 1)
                        for m in range(2):
                            for kc in range(KC):
                                mm = nc.tensor.matmul(bankH[c][:, m * D:(m + 1) * D],
                                                      xb[u][:, m, kc * TI + c * 128:kc * TI + c * 128 + 128],
                                                      wp_sb[:, kc, :], start=(kc == 0), stop=(kc == KC - 1))
                        mm.then_inc(h_ready, 1)

                def transposes(i, u):
                    p = 2 * i + u
                    pe.wait_ge(qn_ready, p + 1)
                    for t in range(3):
                        wait(pe, qT_done, 3 * p + t - 1)
                        for c in range(3):
                            T = CT[c]
                            mm = nc.tensor.transpose(bankT[(u + t) % 2][:, c * 128:c * 128 + T],
                                                     qn[u][0:T, c, TILE_AT[t]:TILE_AT[t] + 128], idn[0:T, 0:T])
                        mm.then_inc(tq_ready, 1)

                def conv(i, u, t):
                    p = 2 * i + u
                    pe.wait_ge(qT_done, 3 * p + t + 1)
                    wait(pe, ca_done, 3 * p + t - 1)
                    for k in range(K):
                        mm = nc.tensor.matmul(bankK[(u + t) % 2][:, 0:L], conv_w[:, t // 2, k, :],
                                              qT[u][:, t, k:k + L], start=(k == 0), stop=(k == K - 1))
                    mm.then_inc(key_ready, 1)

                def values(i, u, c):
                    p = 2 * i + u
                    pe.wait_ge(qT_done, 3 * p + 3)
                    wait(pe, v_evac, 3 * p + c)
                    T, lo = CT[c], PAD + 128 * c
                    nc.tensor.matmul(bankV[0:T, 0:D], qT[u][:, 0, lo:lo + T], ptA_sb[:, :], start=True, stop=False)
                    nc.tensor.matmul(bankV[0:T, D:2 * D], qT[u][:, 1, lo:lo + T], ptA_sb[:, :], start=False, stop=False)
                    nc.tensor.matmul(bankV[0:T, 0:2 * D], qT[u][:, 2, lo:lo + T], ptB_sb[:, :], start=False, stop=True)\
                      .then_inc(v_ready, 1)

                def scores(i, u, c):
                    p = 2 * i + u
                    pe.wait_ge(ca_done, 3 * p + 3)
                    wait(pe, kern_evac, 3 * p + c)
                    T, n = CT[c], HA * K
                    for t in range(3):
                        mm = nc.tensor.matmul(bankN[0:T, t * n:(t + 1) * n], ca[u][:, t, 128 * c:128 * c + T],
                                              (akB_sb if t == 2 else akA_sb)[:, :], start=True, stop=True)
                    mm.then_inc(kern_ready, 1)

                pe.wait_ge(const_loaded, NCONST)
                pe.wait_ge(zeroed, 1)
                patch(0, 0)

                def body(i):
                    for u in range(2):
                        if u == 0:
                            patch(i, 1)
                        elif not (isinstance(i, int) and i == NPAIR // 2 - 1):
                            patch(i + 1, 0)
                        transposes(i, u)
                        if isinstance(i, int) and i == 0 and u == 0:
                            pe.wait_ge(conv_w_ready, 1)
                        for t in range(3):
                            conv(i, u, t)
                            values(i, u, t)
                        for c in range(3):
                            scores(i, u, c)
                peeled(pe, body)

        st = ExitStack()
        with st:
            sb, pb, sem = allocator(st)
            vb = sb("vb", [128, (R + 2 * PAD) * D])
            kb = sb("kb", [128, R * H, K])
            akb_sb = sb("akb_sb", [128, H * K])
            kmax = sb("kmax", [128, R * H])
            ksum = sb("ksum", [128, R * H])
            krec = sb("krec", [128, R * H])
            prod = [sb(f"prod{n}", [128, SL * D]) for n in range(2)]
            xn = sb("xn", [128, R, D])
            stats = sb("stats2", [128, R, 6])
            mv = sb("mean_var2", [128, R, 2])
            vare = sb("var_eps2", [128, R])
            rstd = sb("rstd2", [128, R])
            nmr = sb("minus_mean_rstd", [128, R])
            mhalf = sb("minus_half2", [128, R])
            xTa = [sb(f"xTa{n}", [128, 3 * 128]) for n in range(2)]
            xTb = [sb(f"xTb{n}", [D2, 3 * 128]) for n in range(2)]
            wgA, wgB = sb("wgA", [128, E]), sb("wgB", [D2, E])
            low_sb, ones = sb("lower_sb", [128, 128]), sb("ones", [128, TOPK * E * R])
            rev, val = sb("rev", [128, R * E]), sb("val", [128, R])
            sbase = sb("sbase", [128, TOPK * E])
            lg, lg2, eq = sb("lg", [128, R, E]), sb("lg2", [128, R, E]), sb("eq", [128, R, E])
            m12, i12 = sb("m12", [128, TOPK, R]), sb("i12", [128, TOPK, R])
            oh = sb("onehot", [128, TOPK * E, R])
            ohv = sb("onehot_valid", [128, TOPK * E, R])
            inc = sb("running_count", [128, TOPK * E * R])
            cnt, off, base = sb("cnt", [128, 16]), sb("off", [128, 16]), sb("base", [128, 16])
            pos, pos2 = sb("pos", [128, TOPK * E, R]), sb("pos2", [128, TOPK * E, R])
            posk, slotk = sb("posk", [128, TOPK, R]), sb("slotk", [128, TOPK, R])
            keep = sb("keep", [128, TOPK, R])
            gap, ex, w12 = sb("gap", [128, R]), sb("ex", [128, R]), sb("w12", [128, TOPK, R])
            idx = sb("idx", [128, TOPK, R], i32)

            bankA = [pb(f"bankA{n}") for n in range(2)]
            bankB = [pb(f"bankB{n}") for n in range(2)]
            bankL, bankC = pb("bankL"), pb("bankC")

            c2_loaded = sem("c2_loaded")
            g_loaded = sem("g_loaded")
            step = sem("vector_step")
            sc_ready, sc_exp = sem("sc_ready"), sem("sc_exp")
            win_done = sem("win_done")
            aggr_done, rstd_ready, half_set, eps_added = (sem("aggr_done2"), sem("rstd_ready2"), sem("half_set2"),
                                                          sem("eps_added2"))
            nmr_ready, xn_ready = sem("nmr_ready"), sem("xn_ready")
            tr_ready, tr_evac, lg_ready = sem("tr_ready"), sem("tr_evac"), sem("lg_ready")
            gap_ready, ex_ready = sem("gap_ready"), sem("ex_ready")
            cnt_ready, pre_ready = sem("cnt_ready"), sem("pre_ready")
            idx_ready, scattered = sem("idx_ready"), sem("scattered")

            block = st.enter_context(nc.Block())
            C2 = [(akb_sb[:, :], akb), (wgA[:, :], wg[0:128, :]), (wgB[:, :], wg[128:D, :]), (low_sb[:, :], lower),
                  (rev[:, :], revrank), (val[:, :], valid), (sbase[:, :], slotbase)]
            @block.sync
            def _(sp):
                for dst, src in C2:
                    sp.dma_start(dst, src).then_inc(c2_loaded, 16)

                def load(g):
                    wait(sp, win_done, g)
                    for m in range(GIMG):
                        seg = rows[bass.ds(g * GIMG + m, 1), :, :]
                        ps = slice(m * SEG, (m + 1) * SEG)
                        body = seg[:, PAD:PAD + SEG * R, :].rearrange("b (s r) f -> (b s) r f", r=R)
                        sp.dma_start(vb[ps, 0:R * D].rearrange("p (r d) -> p r d", d=D),
                                     seg[:, 0:SEG * R, 0:D].rearrange("b (s r) f -> (b s) r f", r=R))\
                          .then_inc(g_loaded, 16)
                        sp.dma_start(vb[ps, R * D:(R + 2 * PAD) * D].rearrange("p (r d) -> p r d", d=D),
                                     seg[:, 2 * PAD:2 * PAD + SEG * R, 0:D]
                                     .rearrange("b (s r) f -> (b s) r f", r=R)[:, R - 2 * PAD:R, :])\
                          .then_inc(g_loaded, 16)
                        sp.dma_start(hk_view(g, ps), body[:, :, D:2 * D]).then_inc(g_loaded, 16)
                        sp.dma_start(kb[ps, :, :].rearrange("p (r h) k -> p r (h k)", h=H),
                                     body[:, :, 2 * D:ROW]).then_inc(g_loaded, 16)

                def hk_view(g, ps):
                    return hpost[ps, bass.ds(g * R, R), :]
                load(0)
                with sp.Fori(1, NG) as g:
                    load(g)

            GL = 16 * 4 * GIMG

            @block.gpsimd
            def _(pool):
                nc.gpsimd.memset(mhalf[:, :], -0.5).then_inc(half_set, 1)
                pool.wait_ge(half_set, 1)

                def body(g):
                    pool.wait_ge(aggr_done, g + 1)
                    settled(pool)
                    nc.gpsimd.tensor_scalar(vare[:, :], mv[:, :, 1], EPS, None, ALU.add).then_inc(eps_added, 1)
                    pool.wait_ge(eps_added, g + 1)
                    nc.gpsimd.tensor_tensor(rstd[:, :], vare[:, :], mhalf[:, :], ALU.pow).then_inc(rstd_ready, 1)
                    pool.wait_ge(idx_ready, g + 1)
                    pool.wait_ge(xn_ready, g + 1)
                    settled(pool)
                    for k in range(TOPK):
                        for r in range(R):
                            nc.gpsimd.indirect_dma_start(
                                out=xslots[:, :], out_offset=bass.IndirectOffsetOnAxis(ap=idx[:, k, r:r + 1], axis=0),
                                in_=xn[:, r, :], in_offset=None, bounds_check=NS - 1, oob_is_err=False)\
                              .then_inc(scattered, 16)
                    pool.wait_ge(scattered, 16 * TOPK * R * (g + 1))
                    settled(pool)
                body(0)
                with pool.Fori(1, NG) as g:
                    body(g)

            @block.scalar
            def _(act):
                def body(g):
                    act.wait_ge(sc_ready, g + 1)
                    nc.scalar.activation(kb[:, :, :], kb[:, :, :], ACT.Exp).then_inc(sc_exp, 1)
                    act.wait_ge(nmr_ready, g + 1)
                    wait(act, scattered, 16 * TOPK * R * g)
                    for r in range(R):
                        last = nc.scalar.activation(xn[:, r, :], hpost[:, bass.ds(g * R + r, 1), :], ACT.Identity,
                                                    bias=nmr[:, r:r + 1], scale=rstd[:, r:r + 1])
                    last.then_inc(xn_ready, 1)
                    for q in range(R // 3):
                        act.wait_ge(tr_ready, R // 3 * g + q + 1)
                        nc.scalar.copy(xTa[q % 2][:, :], bankA[q % 2][:, 0:384])
                        nc.scalar.copy(xTb[q % 2][:, :], bankB[q % 2][0:D2, 0:384]).then_inc(tr_evac, 1)
                    act.wait_ge(gap_ready, g + 1)
                    nc.scalar.activation(ex[:, :], gap[:, :], ACT.Exp).then_inc(ex_ready, 1)
                body(0)
                with act.Fori(1, NG) as g:
                    body(g)

            NQ = R // 3

            @block.tensor
            def _(pe):
                pe.wait_ge(c2_loaded, 16 * len(C2))

                def body(g):
                    pe.wait_ge(xn_ready, g + 1)

                    def tr(q):
                        if q >= 2:
                            pe.wait_ge(tr_evac, NQ * g + q - 1)
                        for j in range(3):
                            r = 3 * q + j
                            nc.tensor.transpose(bankA[q % 2][:, j * 128:(j + 1) * 128], xn[:, r, 0:128], idn[:, :])
                            mm = nc.tensor.transpose(bankB[q % 2][0:D2, j * 128:(j + 1) * 128], xn[:, r, 128:D],
                                                     idn[:, :])
                        mm.then_inc(tr_ready, 1)

                    def logit(q):
                        pe.wait_ge(tr_evac, NQ * g + q + 1)
                        for j in range(3):
                            r = 3 * q + j
                            o = bankL[:, r * E:(r + 1) * E]
                            nc.tensor.matmul(o, xTa[q % 2][:, j * 128:(j + 1) * 128], wgA[:, :], start=True, stop=False)
                            mm = nc.tensor.matmul(o, xTb[q % 2][:, j * 128:(j + 1) * 128], wgB[:, :],
                                                  start=False, stop=True)
                        return mm
                    tr(0)
                    for q in range(NQ):
                        if q + 1 < NQ:
                            tr(q + 1)
                        mm = logit(q)
                    mm.then_inc(lg_ready, 1)
                    pe.wait_ge(cnt_ready, g + 1)
                    nc.tensor.matmul(bankC[:, 0:16], low_sb[:, :], cnt[:, :], start=True, stop=True)
                    nc.tensor.matmul(bankC[:, 16:32], ones[:, 0:128], cnt[:, :], start=True, stop=True)\
                      .then_inc(pre_ready, 1)
                body(0)
                with pe.Fori(1, NG) as g:
                    body(g)

            @block.vector
            def _(dve):
                nc.vector.memset(ones[:, :], 1.0)
                nc.vector.memset(base[:, :], 0.0)
                dve.wait_ge(c2_loaded, 16 * len(C2))

                def body(g, steps):
                    n = [0]

                    def done(ins):
                        ins.then_inc(step, 1)
                        n[0] += 1
                        return n[0]

                    def after(k):
                        dve.wait_ge(step, g * steps + k)

                    V = nc.vector
                    dve.wait_ge(g_loaded, GL * (g + 1))
                    kbf = kb[:, :, :].rearrange("p (r h) k -> p r (h k)", h=H)
                    a = done(V.tensor_tensor(kbf, kbf, akb_sb[:, :].unsqueeze(1).to_broadcast([128, R, H * K]), ALU.add))
                    after(a)
                    a = done(V.tensor_reduce(kmax[:, :], kb[:, :, :], AX.X, ALU.max))
                    after(a)
                    V.tensor_tensor(kb[:, :, :], kb[:, :, :], kmax[:, :].unsqueeze(2).to_broadcast([128, R * H, K]),
                                    ALU.subtract).then_inc(sc_ready, 1)
                    dve.wait_ge(sc_exp, g + 1)
                    a = done(V.tensor_reduce(ksum[:, :], kb[:, :, :], AX.X, ALU.add))
                    after(a)
                    a = done(V.reciprocal(krec[:, :], ksum[:, :]))
                    after(a)
                    a = done(V.tensor_tensor(kb[:, :, :], kb[:, :, :],
                                             krec[:, :].unsqueeze(2).to_broadcast([128, R * H, K]), ALU.mult))
                    after(a)
                    turns = [(s, k) for s in range(NSL) for k in range(K)]
                    made = {}
                    added = {}

                    def mult(j):
                        s, k = turns[j]
                        if j >= 2:
                            after(added[j - 2])
                        made[j] = done(V.tensor_tensor(
                            prod[j % 2][:, :].rearrange("p (a d) -> p a d", d=IPG),
                            vb[:, (SL * s + k) * D:(SL * s + k + SL) * D].rearrange("p (a d) -> p a d", d=IPG),
                            kb[:, SL * s * H:SL * (s + 1) * H, k:k + 1].to_broadcast([128, SL * H, IPG]), ALU.mult))

                    def add(j):
                        s, k = turns[j]
                        acc = hpost[:, bass.ds(g * R + SL * s, SL), :].rearrange("p a d -> p (a d)")
                        after(max(made[j], added.get(j - 1, 0)))
                        added[j] = done(V.tensor_tensor(acc, acc, prod[j % 2][:, :], ALU.add))
                    for j in range(len(turns)):
                        mult(j)
                        if j:
                            add(j - 1)
                    add(len(turns) - 1)
                    after(added[len(turns) - 1])
                    settled(dve)
                    for r in range(R):
                        ins = V.bn_stats(stats[:, r, :], hpost[:, bass.ds(g * R + r, 1), :])
                        if r == 0:
                            ins.then_inc(win_done, 1)
                    a = done(ins)
                    after(a)
                    settled(dve)
                    for r in range(R):
                        ins = V.bn_aggr(mv[:, r, :], stats[:, r, :])
                    ins.then_inc(aggr_done, 1)
                    dve.wait_ge(aggr_done, g + 1)
                    dve.wait_ge(rstd_ready, g + 1)
                    wait(dve, xn_ready, g)
                    V.scalar_tensor_tensor(nmr[:, :], mv[:, :, 0], -1.0, rstd[:, :], ALU.mult, ALU.mult)\
                        .then_inc(nmr_ready, 1)
                    dve.wait_ge(lg_ready, g + 1)
                    a = done(V.tensor_copy(lg[:, :, :], bankL[:, 0:R * E].rearrange("p (r e) -> p r e", e=E)))
                    revv = rev[:, :].rearrange("p (r e) -> p r e", e=E)
                    src = lg
                    for k in range(TOPK):
                        after(a)
                        a = done(V.tensor_reduce(m12[:, k, :], src[:, :, :], AX.X, ALU.max))
                        after(a)
                        a = done(V.tensor_tensor(eq[:, :, :], src[:, :, :],
                                                 m12[:, k, :].unsqueeze(2).to_broadcast([128, R, E]), ALU.is_equal))
                        after(a)
                        a = done(V.tensor_tensor(eq[:, :, :], eq[:, :, :], revv, ALU.mult))
                        after(a)
                        a = done(V.tensor_reduce(i12[:, k, :], eq[:, :, :], AX.X, ALU.max))
                        after(a)
                        ohk = oh[:, k * E:(k + 1) * E, :].rearrange("p e r -> p r e")
                        a = done(V.tensor_tensor(ohk, revv, i12[:, k, :].unsqueeze(2).to_broadcast([128, R, E]),
                                                 ALU.is_equal))
                        if k == 0:
                            after(a)
                            a = done(V.scalar_tensor_tensor(lg2[:, :, :], ohk, -BIG, lg[:, :, :], ALU.mult, ALU.add))
                            src = lg2
                    V.tensor_tensor(gap[:, :], m12[:, 1, :], m12[:, 0, :], ALU.subtract).then_inc(gap_ready, 1)
                    after(a)
                    a = done(V.tensor_tensor(ohv[:, :, :], oh[:, :, :],
                                             val[:, :].unsqueeze(1).to_broadcast([128, TOPK * E, R]), ALU.mult))
                    after(a)
                    V.tensor_reduce(cnt[:, :], ohv[:, :, :], AX.X, ALU.add).then_inc(cnt_ready, 1)
                    a = done(V.tensor_tensor_scan(inc[:, :], ones[:, :], ohv[:, :, :].rearrange("p a r -> p (a r)"), 0.0,
                                                  ALU.mult, ALU.add))
                    dve.wait_ge(ex_ready, g + 1)
                    b = done(V.tensor_scalar(gap[:, :], ex[:, :], 1.0, None, ALU.add))
                    after(b)
                    b = done(V.reciprocal(w12[:, 0, :], gap[:, :]))
                    after(b)
                    b = done(V.tensor_tensor(w12[:, 1, :], w12[:, 0, :], ex[:, :], ALU.mult))
                    dve.wait_ge(pre_ready, g + 1)
                    a = done(V.tensor_tensor(off[:, :], bankC[:, 0:16], base[:, :], ALU.add))
                    after(a)
                    ends = inc[:, :].rearrange("p (a r) -> p a r", r=R)[:, 0:TOPK * E - 1, R - 1]
                    V.tensor_tensor(base[:, :], base[:, :], bankC[:, 16:32], ALU.add)
                    a = done(V.tensor_tensor(off[:, 1:16], off[:, 1:16], ends, ALU.subtract))
                    after(a)
                    a = done(V.tensor_tensor(pos[:, :, :], inc[:, :].rearrange("p (a r) -> p a r", r=R),
                                             off[:, :].unsqueeze(2).to_broadcast([128, 16, R]), ALU.add))
                    after(a)
                    done(V.tensor_tensor(pos[:, :, :], pos[:, :, :], ohv[:, :, :], ALU.mult))
                    a = done(V.tensor_tensor(pos2[:, :, :], ohv[:, :, :],
                                             sbase[:, :].unsqueeze(2).to_broadcast([128, 16, R]), ALU.mult))
                    after(a)
                    done(V.tensor_reduce(posk[:, :, :], pos[:, :, :].rearrange("p (k e) r -> p k r e", e=E), AX.X, ALU.add))
                    a = done(V.tensor_reduce(slotk[:, :, :], pos2[:, :, :].rearrange("p (k e) r -> p k r e", e=E), AX.X,
                                             ALU.add))
                    after(a)
                    done(V.tensor_scalar(keep[:, :, :], posk[:, :, :], float(CAP), None, ALU.is_le))
                    a = done(V.tensor_tensor(slotk[:, :, :], slotk[:, :, :], posk[:, :, :], ALU.add))
                    after(a)
                    a = done(V.tensor_tensor(keep[:, :, :], keep[:, :, :],
                                             val[:, :].unsqueeze(1).to_broadcast([128, TOPK, R]), ALU.mult))
                    after(a)
                    a = done(V.scalar_tensor_tensor(slotk[:, :, :], slotk[:, :, :], -float(NS), keep[:, :, :],
                                                    ALU.add, ALU.mult))
                    V.tensor_tensor(wk_all[:, bass.ds(g, 1), :, :].rearrange("p g k r -> p (g k) r"), w12[:, :, :],
                                    keep[:, :, :], ALU.mult)
                    after(a)
                    wait(dve, scattered, 16 * TOPK * R * g)
                    V.tensor_scalar(idx_all[:, bass.ds(g, 1), :, :].rearrange("p g k r -> p (g k) r"), slotk[:, :, :],
                                    float(NS), None, ALU.add)
                    V.tensor_scalar(idx[:, :, :], slotk[:, :, :], float(NS), None, ALU.add).then_inc(idx_ready, 1)
                    return n[0]
                steps = body(0, 0)
                with dve.Fori(1, NG) as g:
                    body(g, steps)

        st = ExitStack()
        with st:
            sb, pb, sem = allocator(st)
            w1a = [sb(f"w1a{n}", [128, 2 * HID]) for n in range(2)]
            w1b = [sb(f"w1b{n}", [D2, 2 * HID]) for n in range(2)]
            w2 = [sb(f"w2_{n}", [128, HID // 128, D]) for n in range(2)]
            NJ, NCH = HID // 128, SLOT_TILE // CHUNK
            xin = [sb(f"xin{n}", [CHUNK, NCH, D]) for n in range(2)]
            xTa = [sb(f"xeTa{n}", [128, SLOT_TILE]) for n in range(2)]
            xTb = [sb(f"xeTb{n}", [D2, SLOT_TILE]) for n in range(2)]
            sg = [sb(f"silu{n}", [128, SLOT_TILE]) for n in range(2)]
            hact = [sb(f"hact{n}", [128, NJ, SLOT_TILE]) for n in range(2)]
            yb = [sb(f"yb{n}", [CHUNK, NCH, D]) for n in range(2)]
            bankA, bankB = pb("bankXA"), pb("bankXB")
            bankU = [pb(f"bankU{n}") for n in range(2)]
            bankG = [pb(f"bankG{n}") for n in range(2)]
            bankY = [pb(f"bankY{n}") for n in range(2)]

            w_loaded = [sem(f"w_loaded{n}") for n in range(2)]
            xin_loaded = [sem(f"xin_loaded{n}") for n in range(2)]
            y_stored = [sem(f"y_stored{n}") for n in range(2)]
            xt_ready, xa_evac, xb_evac = sem("xt_ready"), sem("xa_evac"), sem("xb_evac")
            up_ready, gate_ready, silu_done, act_done = sem("up_ready"), sem("gate_ready"), sem("silu_done"), sem("act_done")
            y_ready, y_evac = sem("y_ready"), sem("y_evac")
            block = st.enter_context(nc.Block())
            BODY = 2 * TPE
            NT = E * TPE

            def rows_of(ap, n):
                return ap[bass.ds(n * SLOT_TILE, SLOT_TILE), :].rearrange("(p j) d -> p j d", j=NCH)

            @block.sync
            def _(sp):
                def load_w(i, ee):
                    e = 2 * i + ee
                    sp.dma_start(w1a[ee][:, :], W1[bass.ds(e, 1), 0:128, :].rearrange("e p f -> p (e f)"))\
                      .then_inc(w_loaded[ee], 16)
                    sp.dma_start(w1b[ee][:, :], W1[bass.ds(e, 1), 128:D, :].rearrange("e p f -> p (e f)"))\
                      .then_inc(w_loaded[ee], 16)
                    sp.dma_start(w2[ee][:, :, :], W2[bass.ds(e, 1), :, :].rearrange("e (j p) d -> p (e j) d", p=128))\
                      .then_inc(w_loaded[ee], 16)

                def body(i):
                    for t in range(BODY):
                        n = BODY * i + t
                        if t % TPE == 2 and not (isinstance(i, int) and i == 0 and t == 2):
                            wait(sp, y_ready, n - 2)
                            ee = t // TPE
                            if ee == 1:
                                load_w(i + 1, 0)
                            else:
                                load_w(i, 1)
                        wait(sp, xt_ready, n - 1)
                        sp.dma_start(xin[t % 2][:, :, :], rows_of(xslots, n)).then_inc(xin_loaded[t % 2], 16)
                load_w(0, 0)
                load_w(0, 1)
                body(0)
                with sp.Fori(1, E // 2 - 1) as i:
                    body(i)

                def last_body(i):
                    for t in range(BODY):
                        n = BODY * i + t
                        if t == 2:
                            wait(sp, y_ready, n - 2)
                            load_w(i, 1)
                        wait(sp, xt_ready, n - 1)
                        sp.dma_start(xin[t % 2][:, :, :], rows_of(xslots, n)).then_inc(xin_loaded[t % 2], 16)
                last_body(E // 2 - 1)

            @block.gpsimd
            def _(pool):
                def body(i):
                    for t in range(BODY):
                        n = BODY * i + t
                        pool.wait_ge(y_evac, n + 1)
                        pool.dma_start(rows_of(yslots, n), yb[t % 2][:, :, :]).then_inc(y_stored[t % 2], 16)
                with pool.Fori(0, E // 2) as i:
                    body(i)
                for v in range(2):
                    pool.wait_ge(y_stored[v], 16 * NT // 2)

            @block.scalar
            def _(act):
                def body(i):
                    for t in range(BODY):
                        n = BODY * i + t
                        act.wait_ge(xt_ready, n + 1)
                        wait(act, act_done, NJ * (n - 1))
                        nc.scalar.copy(xTa[t % 2][:, :], bankA[:, 0:SLOT_TILE]).then_inc(xa_evac, 1)
                        for j in range(NJ):
                            act.wait_ge(gate_ready, NJ * n + j + 1)
                            wait(act, act_done, NJ * n + j - 1)
                            nc.scalar.activation(sg[j % 2][:, :], bankG[j % 2][:, 0:SLOT_TILE], ACT.Silu)\
                              .then_inc(silu_done, 1)
                body(0)
                with act.Fori(1, E // 2) as i:
                    body(i)

            @block.vector
            def _(dve):
                def body(i):
                    for t in range(BODY):
                        n = BODY * i + t
                        dve.wait_ge(xt_ready, n + 1)
                        nc.vector.tensor_copy(xTb[t % 2][:, :], bankB[0:D2, 0:SLOT_TILE]).then_inc(xb_evac, 1)
                        for j in range(NJ):
                            dve.wait_ge(silu_done, NJ * n + j + 1)
                            dve.wait_ge(up_ready, NJ * n + j + 1)
                            if j == 0:
                                wait(dve, y_ready, n - 1)
                            nc.vector.tensor_tensor(hact[t % 2][:, j, :], sg[j % 2][:, :],
                                                    bankU[j % 2][:, 0:SLOT_TILE], ALU.mult).then_inc(act_done, 1)
                            if j == 1:
                                if t > 0:
                                    evac_y(i, t - 1)
                    evac_y(i, BODY - 1)

                def evac_y(i, t):
                    n = BODY * i + t
                    dve.wait_ge(y_ready, n + 1)
                    wait(dve, y_stored[t % 2], 16 * (BODY // 2 * i + t // 2))
                    for a in range(2):
                        last = nc.vector.tensor_copy(yb[t % 2][:, 2 * a:2 * a + 2, :],
                                                     bankY[a][0:CHUNK, 0:2 * D].rearrange("p (j d) -> p j d", j=2))
                    last.then_inc(y_evac, 1)
                body(0)
                with dve.Fori(1, E // 2) as i:
                    body(i)

            @block.tensor
            def _(pe):
                def tr(i, t):
                    n = BODY * i + t
                    pe.wait_ge(xin_loaded[t % 2], 16 * (BODY // 2 * i + t // 2 + 1))
                    wait(pe, xa_evac, n)
                    wait(pe, xb_evac, n)
                    for j in range(NCH):
                        nc.tensor.transpose(bankA[:, j * CHUNK:(j + 1) * CHUNK], xin[t % 2][:, j, 0:128],
                                            idn[0:CHUNK, 0:CHUNK])
                        mm = nc.tensor.transpose(bankB[0:D2, j * CHUNK:(j + 1) * CHUNK], xin[t % 2][:, j, 128:D],
                                                 idn[0:CHUNK, 0:CHUNK])
                    mm.then_inc(xt_ready, 1)

                def up(i, t):
                    n, ee = BODY * i + t, t // TPE
                    if t % TPE == 0:
                        pe.wait_ge(w_loaded[ee], 48 * (i + 1))
                    pe.wait_ge(xa_evac, n + 1)
                    pe.wait_ge(xb_evac, n + 1)
                    for j in range(NJ):
                        for half, bank, ready in ((1, bankG, gate_ready), (0, bankU, up_ready)):
                            if half == 1:
                                wait(pe, act_done, NJ * n + j - 1)
                            lo = half * HID + j * 128
                            nc.tensor.matmul(bank[j % 2][:, 0:SLOT_TILE], w1a[ee][:, lo:lo + 128], xTa[t % 2][:, :],
                                             start=True, stop=False)
                            nc.tensor.matmul(bank[j % 2][:, 0:SLOT_TILE], w1b[ee][:, lo:lo + 128], xTb[t % 2][:, :],
                                             start=False, stop=True).then_inc(ready, 1)

                def down(i, t):
                    n, ee = BODY * i + t, t // TPE
                    pe.wait_ge(act_done, NJ * n + NJ)
                    wait(pe, y_evac, n)
                    for c in range(NCH):
                        for j in range(NJ):
                            mm = nc.tensor.matmul(bankY[c // 2][0:CHUNK, (c % 2) * D:(c % 2 + 1) * D],
                                                  hact[t % 2][:, j, c * CHUNK:(c + 1) * CHUNK], w2[ee][:, j, :],
                                                  start=(j == 0), stop=(j == NJ - 1))
                    mm.then_inc(y_ready, 1)

                def body(i):
                    tr(i, 0)
                    for t in range(BODY):
                        if t + 1 < BODY:
                            tr(i, t + 1)
                        up(i, t)
                        if t:
                            down(i, t - 1)
                    down(i, BODY - 1)
                body(0)
                with pe.Fori(1, E // 2) as i:
                    body(i)

        st = ExitStack()
        with st:
            sb, pb, sem = allocator(st)
            NB = SL
            gb = [sb(f"gathered{n}", [128, TOPK, D]) for n in range(NB)]
            idx = sb("idx4", [128, TOPK, R], i32)
            gathered = [sem(f"gathered_sem{n}") for n in range(NB)]
            idx_ready, added, first_added, out_done = sem("idx4_ready"), sem("added"), sem("first_added"), sem("out_done")
            block = st.enter_context(nc.Block())

            @block.gpsimd
            def _(pool):
                def body(g):
                    pool.wait_ge(idx_ready, g + 1)
                    settled(pool)
                    for r in range(R):
                        wait(pool, added, R * g + r - NB + 1)
                        settled(pool)
                        for k in range(TOPK):
                            nc.gpsimd.indirect_dma_start(
                                out=gb[r % NB][:, k, :], out_offset=None, in_=yslots[:, :],
                                in_offset=bass.IndirectOffsetOnAxis(ap=idx[:, k, r:r + 1], axis=0))\
                              .then_inc(gathered[r % NB], 16)
                body(0)
                with pool.Fori(1, NG) as g:
                    body(g)

            @block.vector
            def _(dve):
                def body(g):
                    wait(dve, added, R * g)
                    nc.vector.tensor_copy(idx[:, :, :], idx_all[:, bass.ds(g, 1), :, :].rearrange("p g k r -> p (g k) r"))\
                      .then_inc(idx_ready, 1)
                    for r in range(R):
                        dve.wait_ge(gathered[r % NB], 32 * (R // NB * g + r // NB + 1))
                        h = hpost[:, bass.ds(g * R + r, 1), :].rearrange("p a d -> p (a d)")
                        for k in range(TOPK):
                            w = wk_all[:, bass.ds(g, 1), k, r:r + 1].rearrange("p g r -> p (g r)")
                            ins = nc.vector.scalar_tensor_tensor(h, gb[r % NB][:, k, :], w, h, ALU.mult, ALU.add)
                            if k == 0:
                                ins.then_inc(first_added, 1)
                                dve.wait_ge(first_added, R * g + r + 1)
                        ins.then_inc(added, 1)
                body(0)
                with dve.Fori(1, NG) as g:
                    body(g)

            @block.sync
            def _(sp):
                def body(g):
                    sp.wait_ge(added, R * (g + 1))
                    for m in range(GIMG):
                        dst = out[bass.ds(g * GIMG + m, 1), :, :]
                        full = (SEG - 1) * R
                        sp.dma_start(dst[:, 0:full, :].rearrange("b (s r) d -> (b s) r d", r=R),
                                     hpost[m * SEG:(m + 1) * SEG - 1, bass.ds(g * R, R), :]).then_inc(out_done, 16)
                        sp.dma_start(dst[:, full:L, :],
                                     hpost[(m + 1) * SEG - 1:(m + 1) * SEG, bass.ds(g * R, RL), :]).then_inc(out_done, 16)
                with sp.Fori(0, NG) as g:
                    body(g)
                sp.wait_ge(out_done, 16 * 2 * B)


def _hilbert():
    pts = []
    for d in range(TI):
        t, x, y, s = d, 0, 0, 1
        while s < CURVE:
            rx = 1 & t // 2
            ry = 1 & (t ^ rx)
            if ry == 0:
                if rx == 1:
                    x, y = s - 1 - x, s - 1 - y
                x, y = y, x
            x, y, t, s = x + s * rx, y + s * ry, t // 4, s * 2
        pts.append((min(x, GRID - 1), min(y, GRID - 1)))
    return np.array(pts)


def _layout(a):
    f = np.float32
    pts = _hilbert()
    xs = np.asarray(a["x"]).reshape(B, CIN, GRID, PATCH, GRID, PATCH)
    xs = xs[:, :, pts[:, 0], :, pts[:, 1], :]
    xs = xs.transpose(1, 2, 3, 4, 0).reshape(B, KC, 128, TI).transpose(0, 2, 1, 3).reshape(B, 128, KC * TI)
    wt = np.asarray(a["L0_tok_W"]).reshape(D, KC, 128).transpose(2, 1, 0)
    dwt = np.asarray(a["L0_attn_dw_w"]).reshape(D, K)
    dwl = np.stack([dwt[:128], np.concatenate([dwt[128:], dwt[128:]])], 1)
    pww, akw = np.asarray(a["L0_attn_pw_w"]), np.asarray(a["L0_attn_ak_w"])
    heads = [list(range(HA)), list(range(HA, H)) * 2]
    pwl = np.zeros((128, 2, 128), f)
    akl = [np.zeros((128, HA * K), f), np.zeros((128, HA * K), f)]
    for t in range(2):
        for n, h in enumerate(heads[t]):
            pwl[n * IPG:(n + 1) * IPG, t, n * IPG:(n + 1) * IPG] = pww[h].T
            akl[t][n * IPG:(n + 1) * IPG, n * K:(n + 1) * K] = akw[h].T
    pb = np.asarray(a["L0_attn_pw_b"])
    pwbl = np.stack([pb[:128], np.concatenate([pb[128:], pb[128:]])], 1)
    ptt = np.asarray(a["L0_attn_pt_w"]).T
    ptBl = np.zeros((128, 2 * D), f)
    ptBl[:D2, :D] = ptt[128:]
    ptBl[D2:, D:] = ptt[128:]

    def rep(v, n=1):
        return np.broadcast_to(np.tile(np.asarray(v), n), (128, n * len(v)))
    revrank = np.broadcast_to(np.tile(E - np.arange(E), R), (128, R * E)).astype(f)
    valid = np.array([[(p % SEG) * R + r < L for r in range(R)] for p in range(128)]).astype(f)
    slotbase = np.broadcast_to(np.array([e * CAPE + k * CAP - 1 for k in range(TOPK) for e in range(E)]), (128, 16))
    return {
        "x": xs, "txt": np.asarray(a["txt"]), "wpatch": wt, "tokb": rep(a["L0_tok_b"], 2), "dw": dwl, "pw": pwl,
        "pwb": pwbl, "akA": akl[0], "akB": akl[1], "akb": rep(a["L0_attn_ak_b"]), "ptA": ptt[:128], "ptB": ptBl,
        "ptb": rep(a["L0_attn_pt_b"], 2), "wg": np.asarray(a["L0_ffn_Wg"]), "W1": np.asarray(a["L0_ffn_W1"]),
        "W2": np.asarray(a["L0_ffn_W2"]), "ident": np.eye(128, dtype=f),
        "lower": np.triu(np.ones((128, 128), f), 1), "revrank": revrank, "valid": valid,
        "slotbase": slotbase.astype(f),
    }


def kernel(**inputs):
    import concourse.bacc as _bacc
    from concourse.bass_utils import run_bass_kernel_spmd as _run

    nc = _bacc.Bacc("TRN2", target_bir_lowering=False, num_devices=1)
    arrays, args = {}, {}
    for name, a in _layout(inputs).items():
        a = np.ascontiguousarray(a)
        arrays[f"in_{name}"] = a
        args[name] = nc.dram_tensor(f"in_{name}", a.shape, mybir.dt.from_np(a.dtype), kind="ExternalInput").ap()
    args["out"] = nc.dram_tensor("out_0", (B, L, D), mybir.dt.float32, kind="ExternalOutput").ap()
    build(nc, **args)
    r = _run(nc, [arrays], core_ids=[0])
    return r.results[0]["out_0"]
```

```python
import numpy as np
import concourse.bass as bass
from concourse import mybir
from contextlib import ExitStack

B, CIN, IMG, PATCH = 32, 3, 224, 16
GRID = IMG // PATCH
CURVE = 16
TI, TT, D = CURVE * CURVE, 77, 192
L = TI + TT
KC = CIN * PATCH * PATCH // 128
H, IPG, K = 12, 16, 9
PAD = (K - 1) // 2
D2 = D - 128
HA = 128 // IPG
HB = H - HA
E, TOPK, HID = 8, 2, 512
CAP = int(1.2 * B * L / E)
SLOT_TILE, CHUNK = 640, 128
HALF = SLOT_TILE // 2
TPE = -(-TOPK * CAP // SLOT_TILE)
CAPE = TPE * SLOT_TILE
CAPK = CAPE // TOPK
MIX, MIXP = CAPK // SLOT_TILE, CAPK % SLOT_TILE * CHUNK // SLOT_TILE
NS = E * CAPE
N = B * L
EPS = 1e-5

NPAIR = B // 2
CT = [128, 128, TT]
ROW = 2 * D + H * K
SEG, R = 16, 21
LROWS = SEG * R + 2 * PAD
GIMG = 128 // SEG
NG = B // GIMG
RL = L - (SEG - 1) * R
SL = 7
NSL = R // SL
BIG = 1e30
NIT = NG + 1
LOB, LOA, META = D, D + D2, 2 * D
XW = META + 8
WSCALE = 64.0


def build(nc, x, txt, wpatch, tokb, dw, pw, pwb, akA, akB, akb, ptA, ptB, ptb, wg, wgpair, W1, W2,
          ident, lower, revrank, valid, slotbase, tokid, out):
    fp32, fp16, i32, u16 = mybir.dt.float32, mybir.dt.float16, mybir.dt.int32, mybir.dt.uint16
    ALU, ACT, AX = mybir.AluOpType, mybir.ActivationFunctionType, mybir.AxisListType

    rows = nc.dram_tensor("token_rows", (B, LROWS, ROW), fp32, kind="Internal").ap()
    xslots = nc.dram_tensor("expert_inputs", (NS, XW), u16, kind="Internal").ap()

    def wait(eng, sem, value):
        if isinstance(value, int) and value <= 0:
            return
        eng.wait_ge(sem, value)

    def settled(eng):
        eng.sem_inc(passed, 1)

    top = ExitStack()
    with top:
        def allocator(stack):
            return (lambda n, s, dt=fp32: stack.enter_context(nc.sbuf_tensor(n, s, dt)),
                    lambda n, dt=fp32: stack.enter_context(nc.psum_tensor(n, [128, 2048 // (4 if dt == fp32 else 2)], dt)),
                    lambda n: stack.enter_context(nc.semaphore(n)))
        sb, _, sem = allocator(top)
        passed = sem("passed")

        idn16 = sb("identity16", [128, 128], fp16)

        st = ExitStack()
        with st:
            sb, pb, sem = allocator(st)
            idn = sb("identity", [128, 128])
            wp_sb = sb("wp_sb", [128, KC, D])
            tokb_sb = sb("tokb_sb", [128, 2 * D])
            dw_sb = sb("dw_sb", [128, 2, K])
            pw_sb = sb("pw_sb", [128, 2, 128])
            pwb_sb = sb("pwb_sb", [128, 2])
            akA_sb = sb("akA_sb", [128, HA * K])
            akB_sb = sb("akB_sb", [128, 2 * HB * K])
            ptA_sb = sb("ptA_sb", [128, D])
            ptB_sb = sb("ptB_sb", [128, 2 * D])
            ptb_sb = sb("ptb_sb", [128, 2 * D])
            conv_w = sb("conv_w", [128, 2, K, 128])
            xb = [sb(f"patches{u}", [128, 2, KC * TI]) for u in range(2)]
            rowb = [sb(f"rowbuf{u}", [128, 3, 2, ROW]) for u in range(2)]
            qn = [sb(f"normed{u}", [128, 3, 2 * D]) for u in range(2)]
            TILE_AT = [0, 2 * 128, 128]
            qT = [sb(f"normedT{u}", [128, 3, L + 2 * PAD]) for u in range(2)]
            ca = [sb(f"conv_attn{u}", [128, 3, L]) for u in range(2)]
            stats = sb("stats", [128, 6, 6])
            mv = sb("mean_var", [128, 6, 2])
            rs = sb("rstd", [128, 2, 6])
            tmp6 = sb("tmp6", [128, 2, 6])
            cst = sb("pool_constants", [128, 3, R])
            zeros = sb("zeros", [128, ROW])
            empty = [sb(f"empty_slots{v}", [CHUNK, SLOT_TILE // CHUNK, XW], u16) for v in range(2)]

            vx = sb("window_values", [128, (R + 2 * PAD) * D])
            kb = sb("kb", [128, R * H, K])
            hg = sb("hidden_group", [128, R, D])
            akb_sb = sb("akb_sb", [128, H * K])
            kmax = sb("kmax", [128, R * H])
            ksum = sb("ksum", [128, R * H])
            krec = sb("krec", [128, R * H])
            prod = [sb(f"prod{n}", [128, SL * D]) for n in range(2)]
            xrow = sb("slot_rows", [128, R, XW], u16)
            xrow16 = xrow[:, :, :].bitcast(fp16)
            stats2 = sb("stats2", [128, R, 6])
            mv2 = sb("mean_var2", [128, R, 2])
            rs2 = sb("rstd2", [128, 2, R])
            tmp21 = sb("tmp21", [128, 2, R])
            xTr = [sb(f"xTr{n}", [128, 3 * 128]) for n in range(2)]
            wgA, wgP, wgC = sb("wgA", [128, E]), sb("wgP", [128, 2 * E]), sb("wgC", [128, E])
            low_sb, ones = sb("lower_sb", [128, 128]), sb("ones", [128, TOPK * E * R])
            rev, val, tid = sb("rev", [128, R * E]), sb("val", [128, R]), sb("token_numbers", [128, R])
            sbase = sb("sbase", [128, TOPK * E])
            lg, lg2, eq = sb("lg", [128, R, E]), sb("lg2", [128, R, E]), sb("eq", [128, R, E])
            m12, i12 = sb("m12", [128, TOPK, R]), sb("i12", [128, TOPK, R])
            oh = sb("onehot", [128, TOPK * E, R])
            ohv = sb("onehot_valid", [128, TOPK * E, R])
            inc = sb("running_count", [128, TOPK * E * R])
            cnt, off, base = sb("cnt", [128, 16]), sb("off", [128, 16]), sb("base", [128, 16])
            pos, pos2 = sb("pos", [128, TOPK * E, R]), sb("pos2", [128, TOPK * E, R])
            posk, slotk = sb("posk", [128, TOPK, R]), sb("slotk", [128, TOPK, R])
            keep = sb("keep", [128, TOPK, R])
            gap, ex, w12 = sb("gap", [128, R]), sb("ex", [128, R]), sb("w12", [128, TOPK, R])
            idx = sb("idx", [128, TOPK, R], i32)

            bankH = [pb(f"bankH{c}") for c in range(2)]
            bankT = [pb(f"bankT{c}") for c in range(2)]
            bankK = [pb(f"bankK{c}") for c in range(2)]
            bankV = pb("bankV")
            bankN = pb("bankN")

            const_loaded = sem("const_loaded")
            zeroed = sem("zeroed")
            empty_set = sem("empty_set")
            fill_done = sem("fill_done")
            x_loaded = [sem(f"x_loaded{u}") for u in range(2)]
            txt_loaded = [sem(f"txt_loaded{u}") for u in range(2)]
            row_stored = [sem(f"row_stored{u}") for u in range(2)]
            conv_w_ready = sem("conv_w_ready")
            h_ready = sem("h_ready")
            h_in_rows = sem("h_in_rows")
            stats_done = sem("stats_done")
            aggr_done = sem("aggr_done")
            pool_step = sem("pool_step")
            pool_step2 = sem("pool_step2")
            cst_set = sem("cst_set")
            qn_ready = sem("qn_ready")
            tq_ready = sem("tq_ready")
            qT_done = sem("qT_done")
            key_ready = sem("key_ready")
            ca_done = sem("ca_done")
            v_ready = sem("v_ready")
            v_evac = sem("v_evac")
            kern_ready = sem("kern_ready")
            kern_evac = sem("kern_evac")

            vk_loaded = sem("vk_loaded")
            hg_loaded = sem("hg_loaded")
            step = sem("vector_step")
            sc_ready, sc_exp = sem("sc_ready"), sem("sc_exp")
            window_done = sem("window_done")
            aggr2_done = sem("aggr2_done")
            xn_ready, xh_ready, xl_ready = sem("xn_ready"), sem("xh_ready"), sem("xl_ready")
            tr_ready, tr_evac, lg_ready, lg_read = sem("tr_ready"), sem("tr_evac"), sem("lg_ready"), sem("lg_read")
            routed = sem("routed")
            gap_ready, ex_ready = sem("gap_ready"), sem("ex_ready")
            cnt_ready, pre_ready, pre_read = sem("cnt_ready"), sem("pre_ready"), sem("pre_read")
            idx_ready, scattered, rows_sent = sem("idx_ready"), sem("scattered"), sem("rows_sent")
            h_stored = [sem(f"h_stored{s}") for s in range(NSL)]

            block = st.enter_context(nc.Block())

            CONSTS = [(idn[:, :], ident), (wp_sb[:, :, :], wpatch), (tokb_sb[:, :], tokb), (dw_sb[:, :, :], dw),
                      (pw_sb[:, :, :], pw), (pwb_sb[:, :], pwb), (akA_sb[:, :], akA), (akB_sb[:, :], akB),
                      (ptA_sb[:, :], ptA), (ptB_sb[:, :], ptB), (ptb_sb[:, :], ptb),
                      (akb_sb[:, :], akb), (wgA[:, :], wg[0:128, :]), (wgP[:, :], wgpair), (wgC[:, :], wg[D2:D, :]), (low_sb[:, :], lower),
                      (rev[:, :], revrank), (val[:, :], valid), (sbase[:, :], slotbase), (tid[:, :], tokid)]
            NCONST = 16 * len(CONSTS)
            NFILL = 3 + 2 * E
            NPOOL = 4
            PAIRS = [min(2 * n, R - 2) for n in range(-(-R // 2))]
            NQ = len(PAIRS)
            GI3 = 2 * (GIMG // 2 - 1)
            NSC = TOPK * R
            PPI = GIMG // 2

            def first(it, n=0):
                return isinstance(it, int) and it == n

            def turns_of(eng, body, peel):
                for it in range(peel):
                    body(it)
                with eng.Fori(peel, NIT - 1) as it:
                    body(it)
                body(NIT - 1)

            def last_pair(it, q):
                return first(it, NG - 1) and q == PPI - 1

            @block.sync
            def _(sp):
                def load_x(j, u):
                    sp.dma_start(xb[u][:, :, :], x[bass.ds(4 * j + 2 * u, 2), :, :].rearrange("b p f -> p b f"))\
                      .then_inc(x_loaded[u], 16)

                def load_txt(j, u):
                    wait(sp, row_stored[u], 64 * j)
                    sp.dma_start(rowb[u][0:TT, 2, :, D:2 * D],
                                 txt[bass.ds(4 * j + 2 * u, 2), :, :].rearrange("b t d -> t b d"))\
                      .then_inc(txt_loaded[u], 16)

                def store(j, u):
                    p = 2 * j + u
                    sp.wait_ge(v_evac, 3 * p + 3)
                    sp.wait_ge(kern_evac, 3 * p + 3)
                    for m in range(2):
                        img = rows[bass.ds(2 * p + m, 1), :, :]
                        sp.dma_start(img[:, PAD:PAD + TI, :].rearrange("b (c p) f -> p (b c) f", p=128),
                                     rowb[u][:, 0:2, m, :]).then_inc(row_stored[u], 16)
                        sp.dma_start(img[:, PAD + TI:PAD + L, :].rearrange("b p f -> p (b f)"),
                                     rowb[u][0:TT, 2, m, :]).then_inc(row_stored[u], 16)

                def load_vk(g, lo, hi):
                    sp.wait_ge(row_stored[0], 64 * (2 * g + 2 if hi > 4 else 2 * g + 1))
                    sp.wait_ge(row_stored[1], 64 * (2 * g + 2 if hi > 6 else 2 * g + 1))
                    wait(sp, window_done, NSL * g)
                    for m in range(lo, hi):
                        seg = rows[bass.ds(g * GIMG + m, 1), :, :]
                        ps = slice(m * SEG, (m + 1) * SEG)
                        body = seg[:, PAD:PAD + SEG * R, :].rearrange("b (s r) f -> (b s) r f", r=R)
                        sp.dma_start(kb[ps, :, :].rearrange("p (r h) k -> p r (h k)", h=H),
                                     body[:, :, 2 * D:ROW]).then_inc(vk_loaded, 16)
                        sp.dma_start(vx[ps, 0:R * D].rearrange("p (r d) -> p r d", d=D),
                                     seg[:, 0:SEG * R, 0:D].rearrange("b (s r) f -> (b s) r f", r=R))\
                          .then_inc(vk_loaded, 16)
                        sp.dma_start(vx[ps, R * D:(R + 2 * PAD) * D].rearrange("p (r d) -> p r d", d=D),
                                     seg[:, 2 * PAD:2 * PAD + SEG * R, 0:D]
                                     .rearrange("b (s r) f -> (b s) r f", r=R)[:, R - 2 * PAD:R, :])\
                          .then_inc(vk_loaded, 16)

                def load_hidden(g):
                    wait(sp, tr_ready, NQ * g)
                    wait(sp, xh_ready, NSL * g)
                    wait(sp, xl_ready, NSL * g)
                    for m in range(GIMG):
                        seg = rows[bass.ds(g * GIMG + m, 1), :, :]
                        sp.dma_start(hg[m * SEG:(m + 1) * SEG, :, :],
                                     seg[:, PAD:PAD + SEG * R, D:2 * D].rearrange("b (s r) f -> (b s) r f", r=R))\
                          .then_inc(hg_loaded, 16)

                def store_slice(g, s):
                    sp.wait_ge(window_done, NSL * g + s + 1)
                    full = (SEG - 1) * R
                    for m in range(GIMG):
                        dst = out[bass.ds((g * GIMG + m) * L, L), :]
                        sp.dma_start(dst[0:full, :].rearrange("(s r) d -> s r d", r=R)[:, s * SL:(s + 1) * SL, :],
                                     hg[m * SEG:(m + 1) * SEG - 1, s * SL:(s + 1) * SL, :]).then_inc(h_stored[s], 16)
                        n = min((s + 1) * SL, RL) - s * SL
                        sp.dma_start(dst[full + s * SL:full + s * SL + n, :].unsqueeze(0),
                                     hg[(m + 1) * SEG - 1:(m + 1) * SEG, s * SL:s * SL + n, :]).then_inc(h_stored[s], 16)

                load_x(0, 0)
                for dst, src in CONSTS:
                    sp.dma_start(dst, src).then_inc(const_loaded, 16)
                load_x(0, 1)
                sp.wait_ge(zeroed, 1)
                for u in range(2):
                    load_txt(0, u)
                sp.wait_ge(h_ready, 2)
                load_x(1, 0)

                def body(it):
                    pairs, groups = not first(it, NIT - 1), not first(it)
                    for q in range(PPI):
                        if pairs:
                            j, u = 2 * it + q // 2, q % 2
                            if not (first(it, NG - 1) and q >= 1):
                                sp.wait_ge(h_ready, 2 * (PPI * it + q + 1) + 2)
                                load_x(j + 1 + u, 1 - u)
                            if q == 3:
                                if first(it):
                                    sp.wait_ge(fill_done, 16 * NFILL)
                                load_vk(it, 0, GI3)
                        if groups and q == 1:
                            store_slice(it - 1, 0)
                        if pairs:
                            store(j, u)
                            if not (first(it, NG - 1) and q >= 2):
                                load_txt(j + 1, u)
                        if groups and q == 1:
                            store_slice(it - 1, 1)
                        if groups and q == 2:
                            store_slice(it - 1, 2)
                    if pairs:
                        load_vk(it, GI3, GIMG)
                        load_hidden(it)
                for it in range(2):
                    body(it)
                with sp.Fori(2, NIT - 2) as it:
                    body(it)
                body(NG - 1)
                body(NIT - 1)
                for s in range(NSL):
                    sp.wait_ge(h_stored[s], 16 * 2 * GIMG * NG)

            @block.gpsimd
            def _(pool):
                for k, c in enumerate((-0.5, EPS, -1.0)):
                    nc.gpsimd.memset(cst[:, k, :], c).then_inc(cst_set, 1)
                pool.wait_ge(zeroed, 1)
                for v in range(2):
                    nc.gpsimd.iota(empty[v][:, :, :].bitcast(i32)[:, :, META // 2:META // 2 + 1],
                                   [[1, SLOT_TILE // CHUNK]], base=N + v * SLOT_TILE,
                                   channel_multiplier=SLOT_TILE // CHUNK).then_inc(empty_set, 1)
                pool.wait_ge(cst_set, 3)

                def layer_norm(mean, var, tmp, res, n, sem_, at):
                    TTn = nc.gpsimd.tensor_tensor
                    TTn(tmp[:, 0, :], var, cst[:, 1, 0:n], ALU.add).then_inc(sem_, 1)
                    pool.wait_ge(sem_, at + 1)
                    TTn(res[:, 0, :], tmp[:, 0, :], cst[:, 0, 0:n], ALU.pow).then_inc(sem_, 1)
                    pool.wait_ge(sem_, at + 2)
                    TTn(tmp[:, 1, :], mean, res[:, 0, :], ALU.mult).then_inc(sem_, 1)
                    pool.wait_ge(sem_, at + 3)
                    TTn(res[:, 1, :], tmp[:, 1, :], cst[:, 2, 0:n], ALU.mult).then_inc(sem_, 1)

                def pair_norm(p):
                    pool.wait_ge(aggr_done, p + 1)
                    wait(pool, qn_ready, p)
                    layer_norm(mv[:, :, 0], mv[:, :, 1], tmp6, rs, 6, pool_step, NPOOL * p)

                def group_norm(g, s):
                    ss = slice(s * SL, (s + 1) * SL)
                    pool.wait_ge(aggr2_done, NSL * g + s + 1)
                    layer_norm(mv2[:, ss, 0], mv2[:, ss, 1], tmp21[:, :, ss], rs2[:, :, ss], SL, pool_step2,
                               NPOOL * (NSL * g + s))

                def low_parts(g, s):
                    ss = slice(s * SL, (s + 1) * SL)
                    pool.wait_ge(xh_ready, NSL * g + s + 1)
                    nc.gpsimd.tensor_tensor(xrow16[:, ss, LOB:LOA], hg[:, ss, 128:D], xrow16[:, ss, 128:D], ALU.subtract)
                    nc.gpsimd.tensor_tensor(xrow16[:, ss, LOA:META], hg[:, ss, 0:128], xrow16[:, ss, 0:128], ALU.subtract)\
                        .then_inc(xl_ready, 1)

                def scatter(g, part):
                    if part == 0:
                        pool.wait_ge(idx_ready, g + 1)
                        pool.wait_ge(xl_ready, NSL * g + NSL)
                        settled(pool)
                    for n in range(part * NSC // 3, (part + 1) * NSC // 3):
                        k, r = n // R, n % R
                        nc.gpsimd.indirect_dma_start(
                            out=xslots[:, :], out_offset=bass.IndirectOffsetOnAxis(ap=idx[:, k, r:r + 1], axis=0),
                            in_=xrow[:, r, :], in_offset=None, bounds_check=NS - 1, oob_is_err=False)\
                            .then_inc(scattered, 16)
                    if part == 2:
                        pool.wait_ge(scattered, 16 * NSC * (g + 1))
                        pool.sem_inc(rows_sent, 1)

                pair_norm(0)

                def body(it):
                    older = not first(it) and not first(it, 1)
                    for q in range(PPI):
                        g = it - 1
                        if older and q < 2:
                            scatter(it - 2, 2 * q)
                        if q == 1 and not first(it):
                            group_norm(g, 0)
                        if not first(it, NIT - 1) and not last_pair(it, q):
                            pair_norm(PPI * it + q + 1)
                        if older and q == 0:
                            scatter(it - 2, 1)
                        if q == 1 and not first(it):
                            group_norm(g, 1)
                            low_parts(g, 0)
                        if q == 2 and not first(it):
                            low_parts(g, 1)
                            group_norm(g, 2)
                            low_parts(g, 2)
                for it in range(2):
                    body(it)
                with pool.Fori(2, NIT - 2) as it:
                    body(it)
                body(NG - 1)
                body(NIT - 1)
                for part in range(3):
                    scatter(NG - 1, part)

            @block.scalar
            def _(act):
                act.wait_ge(zeroed, 1)
                act.dma_start(rows[:, 0:PAD, :], zeros[0:B, :].unsqueeze(1).to_broadcast([B, PAD, ROW]))\
                   .then_inc(fill_done, 16)
                tail = LROWS - PAD - L
                act.dma_start(rows[:, PAD + L:LROWS, :], zeros[0:B, :].unsqueeze(1).to_broadcast([B, tail, ROW]))\
                   .then_inc(fill_done, 16)
                act.dma_start(out[N:N + 2 * SLOT_TILE, :].rearrange("(p j) d -> p j d", p=CHUNK),
                              zeros[0:CHUNK, 0:D].unsqueeze(1).to_broadcast([CHUNK, 2 * SLOT_TILE // CHUNK, D]))\
                   .then_inc(fill_done, 16)
                act.wait_ge(empty_set, 2)
                tiles = xslots.rearrange("(e t p j) f -> e p t (j f)", t=TPE, p=CHUNK, e=E)
                for e in range(E):
                    for v in range(2):
                        act.dma_start(tiles[e][:, v::2, :], empty[v][:, :, :].rearrange("p j f -> p (j f)").unsqueeze(1)
                                      .to_broadcast([CHUNK, (TPE + 1 - v) // 2, SLOT_TILE // CHUNK * XW]))\
                           .then_inc(fill_done, 16)

                def normalise(p, u):
                    act.wait_ge(pool_step, NPOOL * (p + 1))
                    wait(act, tq_ready, 3 * p - 3)
                    for c in (0, 1, 2):
                        for m in range(2):
                            parts = [(0, 0, D)] if m == 0 else [(2 * 128, 0, 128), (D, 128, D2)]
                            for to, ch, n in parts:
                                last = nc.scalar.activation(
                                    qn[u][:, c, to:to + n], rowb[u][:, c, m, D + ch:D + ch + n], ACT.Identity,
                                    bias=rs[:, 1, 2 * c + m:2 * c + m + 1], scale=rs[:, 0, 2 * c + m:2 * c + m + 1])
                    last.then_inc(qn_ready, 1)

                def tiles_out(p, u):
                    for t in range(3):
                        act.wait_ge(tq_ready, 3 * p + t + 1)
                        if t == 0:
                            wait(act, ca_done, 3 * p - 3)
                        nc.scalar.copy(qT[u][:, t, PAD:PAD + L], bankT[(u + t) % 2][:, 0:L]).then_inc(qT_done, 1)

                def scores_out(p, j, u):
                    for c in range(3):
                        act.wait_ge(kern_ready, 3 * p + c + 1)
                        if c == 0:
                            wait(act, row_stored[u], 64 * j)
                        T = CT[c]
                        nc.scalar.copy(rowb[u][0:T, c, :, 2 * D:2 * D + HA * K],
                                       bankN[0:T, 0:2 * HA * K].rearrange("p (m k) -> p m k", m=2))
                        nc.scalar.copy(rowb[u][0:T, c, :, 2 * D + HA * K:ROW],
                                       bankN[0:T, 2 * HA * K:2 * H * K].rearrange("p (m k) -> p m k", m=2))\
                          .then_inc(kern_evac, 1)

                def normalise_slice(g, s):
                    act.wait_ge(pool_step2, NPOOL * (NSL * g + s + 1))
                    act.wait_ge(h_stored[s], 16 * 2 * GIMG * (g + 1))
                    for r in range(s * SL, (s + 1) * SL):
                        last = nc.scalar.activation(hg[:, r, :], hg[:, r, :], ACT.Identity,
                                                    bias=rs2[:, 1, r:r + 1], scale=rs2[:, 0, r:r + 1])
                    last.then_inc(xn_ready, 1)
                    act.wait_ge(xn_ready, NSL * g + s + 1)
                    if s == 0:
                        wait(act, rows_sent, g)
                    ss = slice(s * SL, (s + 1) * SL)
                    nc.scalar.copy(xrow16[:, ss, 0:D], hg[:, ss, :]).then_inc(xh_ready, 1)

                def routing_out(g):
                    for n in range(NQ):
                        act.wait_ge(tr_ready, NQ * g + n + 1)
                        if n == 0:
                            wait(act, lg_ready, g)
                        if n > 1:
                            act.wait_ge(routed, (NQ - 1) * g + n - 1)
                        nc.scalar.copy(xTr[n % 2][:, :], bankT[n % 2][:, 0:384]).then_inc(tr_evac, 1)

                def body(it):
                    pairs, groups = not first(it, NIT - 1), not first(it)
                    for q in range(PPI):
                        p, j, u = PPI * it + q, 2 * it + q // 2, q % 2
                        more = pairs and not last_pair(it, q)
                        if more:
                            normalise(p + 1, 1 - u)
                        if q == 0 and groups:
                            act.wait_ge(sc_ready, it)
                            nc.scalar.activation(kb[:, :, :], kb[:, :, :], ACT.Exp).then_inc(sc_exp, 1)
                        if q == 3 and groups:
                            routing_out(it - 1)
                            act.wait_ge(gap_ready, it)
                            nc.scalar.activation(ex[:, :], gap[:, :], ACT.Exp).then_inc(ex_ready, 1)
                        if more:
                            tiles_out(p + 1, 1 - u)
                        if pairs:
                            scores_out(p, j, u)
                        if groups and q == 1:
                            normalise_slice(it - 1, 0)
                            normalise_slice(it - 1, 1)
                        if groups and q == 2:
                            normalise_slice(it - 1, 2)
                normalise(0, 0)
                tiles_out(0, 0)
                for it in range(2):
                    body(it)
                with act.Fori(2, NIT - 2) as it:
                    body(it)
                body(NG - 1)
                body(NIT - 1)

            @block.vector
            def _(dve):
                V = nc.vector
                for u in range(2):
                    V.memset(qT[u][:, :, :], 0.0)
                    V.memset(rowb[u][:, 2, :, D:2 * D], 0.0)
                V.memset(xrow[:, :, META:XW], 0)
                V.memset(empty[0][:, :, :], 0)
                V.memset(empty[1][:, :, :], 0)
                V.memset(ones[:, :], 1.0)
                V.memset(base[:, :], 0.0)
                V.memset(zeros[:, :], 0.0).then_inc(zeroed, 1)
                dve.wait_ge(const_loaded, NCONST)
                V.tensor_copy(idn16[:, :], idn[:, :])
                for t in range(2):
                    for k in range(K):
                        last = V.tensor_scalar(conv_w[:, t, k, :], pw_sb[:, t, :], dw_sb[:, t, k:k + 1], None, ALU.mult)
                last.then_inc(conv_w_ready, 1)

                def norm(p, j, u):
                    wait(dve, row_stored[u], 64 * j)
                    for c in range(2):
                        dve.wait_ge(h_ready, 2 * p + c + 1)
                        V.tensor_tensor(rowb[u][:, c, :, D:2 * D],
                                        bankH[c][:, 0:2 * D].rearrange("p (m d) -> p m d", m=2),
                                        tokb_sb[:, :].rearrange("p (m d) -> p m d", m=2), ALU.add)\
                            .then_inc(h_in_rows, 1)
                    dve.wait_ge(txt_loaded[u], 16 * (j + 1))
                    dve.wait_ge(h_in_rows, 2 * p + 2)
                    for c in (2, 0, 1):
                        for m in range(2):
                            last = V.bn_stats(stats[:, 2 * c + m, :], rowb[u][:, c, m, D:2 * D])
                    last.then_inc(stats_done, 1)
                    dve.wait_ge(stats_done, p + 1)
                    wait(dve, pool_step, NPOOL * p)
                    settled(dve)
                    for n in range(6):
                        last = V.bn_aggr(mv[:, n, :], stats[:, n, :])
                    last.then_inc(aggr_done, 1)

                def attend(p, u, t):
                    dve.wait_ge(key_ready, 3 * p + t + 1)
                    wait(dve, kern_ready, 3 * p - 3)
                    V.scalar_tensor_tensor(ca[u][:, t, :], bankK[(u + t) % 2][:, 0:L],
                                           pwb_sb[:, t // 2:t // 2 + 1], qT[u][:, t, PAD:PAD + L],
                                           ALU.add, ALU.mult).then_inc(ca_done, 1)
                    T = CT[t]
                    dve.wait_ge(v_ready, 3 * p + t + 1)
                    V.tensor_tensor(rowb[u][0:T, t, :, 0:D],
                                    bankV[0:T, 0:2 * D].rearrange("p (m d) -> p m d", m=2),
                                    ptb_sb[0:T, :].rearrange("p (m d) -> p m d", m=2), ALU.add)\
                        .then_inc(v_evac, 1)

                counted = [0]
                per_group = []

                def done(ins):
                    ins.then_inc(step, 1)
                    counted[0] += 1
                    return counted[0]

                def after(g, k):
                    dve.wait_ge(step, g * per_group[0] + k if per_group else k)

                def softmax_top(g):
                    counted[0] = 0
                    dve.wait_ge(vk_loaded, 16 * 3 * GIMG * (g + 1))
                    kbf = kb[:, :, :].rearrange("p (r h) k -> p r (h k)", h=H)
                    a = done(V.tensor_tensor(kbf, kbf, akb_sb[:, :].unsqueeze(1).to_broadcast([128, R, H * K]), ALU.add))
                    after(g, a)
                    a = done(V.tensor_reduce(kmax[:, :], kb[:, :, :], AX.X, ALU.max))
                    after(g, a)
                    V.tensor_tensor(kb[:, :, :], kb[:, :, :], kmax[:, :].unsqueeze(2).to_broadcast([128, R * H, K]),
                                    ALU.subtract).then_inc(sc_ready, 1)

                def softmax_end(g):
                    dve.wait_ge(sc_exp, g + 1)
                    a = done(V.tensor_reduce(ksum[:, :], kb[:, :, :], AX.X, ALU.add))
                    after(g, a)
                    a = done(V.reciprocal(krec[:, :], ksum[:, :]))
                    after(g, a)
                    a = done(V.tensor_tensor(kb[:, :, :], kb[:, :, :],
                                             krec[:, :].unsqueeze(2).to_broadcast([128, R * H, K]), ALU.mult))
                    after(g, a)

                def window(g, s):
                    acc = hg[:, SL * s:SL * (s + 1), :].rearrange("p a d -> p (a d)")
                    made, added = {}, {}

                    def mult(k):
                        if k >= 2:
                            after(g, added[k - 2])
                        made[k] = done(V.tensor_tensor(
                            prod[k % 2][:, :].rearrange("p (a d) -> p a d", d=IPG),
                            vx[:, (SL * s + k) * D:(SL * s + k + SL) * D].rearrange("p (a d) -> p a d", d=IPG),
                            kb[:, SL * s * H:SL * (s + 1) * H, k:k + 1].to_broadcast([128, SL * H, IPG]), ALU.mult))

                    def add(k):
                        after(g, max(made[k], added.get(k - 1, 0)))
                        added[k] = done(V.tensor_tensor(acc, acc, prod[k % 2][:, :], ALU.add))
                    mult(0)
                    yield
                    for k in range(1, K):
                        mult(k)
                        yield
                        if s == 0 and k == 1:
                            dve.wait_ge(hg_loaded, 16 * GIMG * (g + 1))
                        add(k - 1)
                        yield
                    add(K - 1)
                    after(g, added[K - 1])
                    yield

                def slice_stats(g, s):
                    settled(dve)
                    for r in range(s * SL, (s + 1) * SL):
                        ins = V.bn_stats(stats2[:, r, :], hg[:, r, :])
                        if r == s * SL:
                            ins.then_inc(window_done, 1)
                    a = done(ins)
                    after(g, a)
                    settled(dve)
                    for r in range(s * SL, (s + 1) * SL):
                        ins = V.bn_aggr(mv2[:, r, :], stats2[:, r, :])
                    ins.then_inc(aggr2_done, 1)

                def top_two(g):
                    dve.wait_ge(lg_ready, g + 1)
                    a = done(V.tensor_copy(lg[:, :, :], bankN[:, 0:R * E].rearrange("p (r e) -> p r e", e=E)))
                    revv = rev[:, :].rearrange("p (r e) -> p r e", e=E)
                    src = lg
                    for k in range(TOPK):
                        after(g, a)
                        ins = V.tensor_reduce(m12[:, k, :], src[:, :, :], AX.X, ALU.max)
                        a = done(ins)
                        after(g, a)
                        if k == 0:
                            dve.sem_inc(lg_read, 1)
                        a = done(V.tensor_tensor(eq[:, :, :], src[:, :, :],
                                                 m12[:, k, :].unsqueeze(2).to_broadcast([128, R, E]), ALU.is_equal))
                        after(g, a)
                        a = done(V.tensor_tensor(eq[:, :, :], eq[:, :, :], revv, ALU.mult))
                        after(g, a)
                        a = done(V.tensor_reduce(i12[:, k, :], eq[:, :, :], AX.X, ALU.max))
                        after(g, a)
                        ohk = oh[:, k * E:(k + 1) * E, :].rearrange("p e r -> p r e")
                        a = done(V.tensor_tensor(ohk, revv, i12[:, k, :].unsqueeze(2).to_broadcast([128, R, E]),
                                                 ALU.is_equal))
                        if k == 0:
                            after(g, a)
                            a = done(V.scalar_tensor_tensor(lg2[:, :, :], ohk, -BIG, lg[:, :, :], ALU.mult, ALU.add))
                            src = lg2
                    V.tensor_tensor(gap[:, :], m12[:, 1, :], m12[:, 0, :], ALU.subtract).then_inc(gap_ready, 1)
                    after(g, a)
                    a = done(V.tensor_tensor(ohv[:, :, :], oh[:, :, :],
                                             val[:, :].unsqueeze(1).to_broadcast([128, TOPK * E, R]), ALU.mult))
                    after(g, a)
                    V.tensor_reduce(cnt[:, :], ohv[:, :, :], AX.X, ALU.add).then_inc(cnt_ready, 1)
                    a = done(V.tensor_tensor_scan(inc[:, :], ones[:, :], ohv[:, :, :].rearrange("p a r -> p (a r)"), 0.0,
                                                  ALU.mult, ALU.add))

                def places(g):
                    dve.wait_ge(ex_ready, g + 1)
                    b = done(V.tensor_scalar(gap[:, :], ex[:, :], 1.0, None, ALU.add))
                    after(g, b)
                    b = done(V.reciprocal(w12[:, 0, :], gap[:, :]))
                    after(g, b)
                    done(V.tensor_tensor(w12[:, 1, :], w12[:, 0, :], ex[:, :], ALU.mult))
                    dve.wait_ge(pre_ready, g + 1)
                    done(V.tensor_tensor(off[:, :], bankV[:, 0:16], base[:, :], ALU.add))
                    a = done(V.tensor_tensor(base[:, :], base[:, :], bankV[:, 16:32], ALU.add))
                    after(g, a)
                    ends = inc[:, :].rearrange("p (a r) -> p a r", r=R)[:, 0:TOPK * E - 1, R - 1]
                    ins = V.tensor_tensor(off[:, 1:16], off[:, 1:16], ends, ALU.subtract)
                    dve.sem_inc(pre_read, 1)
                    a = done(ins)
                    after(g, a)
                    a = done(V.tensor_tensor(pos[:, :, :], inc[:, :].rearrange("p (a r) -> p a r", r=R),
                                             off[:, :].unsqueeze(2).to_broadcast([128, 16, R]), ALU.add))
                    after(g, a)
                    done(V.tensor_tensor(pos[:, :, :], pos[:, :, :], ohv[:, :, :], ALU.mult))
                    a = done(V.tensor_tensor(pos2[:, :, :], ohv[:, :, :],
                                             sbase[:, :].unsqueeze(2).to_broadcast([128, 16, R]), ALU.mult))
                    after(g, a)
                    done(V.tensor_reduce(posk[:, :, :], pos[:, :, :].rearrange("p (k e) r -> p k r e", e=E), AX.X, ALU.add))
                    a = done(V.tensor_reduce(slotk[:, :, :], pos2[:, :, :].rearrange("p (k e) r -> p k r e", e=E), AX.X,
                                             ALU.add))
                    after(g, a)
                    done(V.tensor_scalar(keep[:, :, :], posk[:, :, :], float(CAP), None, ALU.is_le))
                    a = done(V.tensor_tensor(slotk[:, :, :], slotk[:, :, :], posk[:, :, :], ALU.add))
                    after(g, a)
                    a = done(V.tensor_tensor(keep[:, :, :], keep[:, :, :],
                                             val[:, :].unsqueeze(1).to_broadcast([128, TOPK, R]), ALU.mult))
                    after(g, a)
                    a = done(V.scalar_tensor_tensor(slotk[:, :, :], slotk[:, :, :], -float(NS), keep[:, :, :],
                                                    ALU.add, ALU.mult))
                    wait(dve, rows_sent, g)
                    V.tensor_copy(xrow[:, :, :].bitcast(fp32)[:, :, META // 2 + 1:META // 2 + 3],
                                  w12[:, :, :].rearrange("p k r -> p r k"))
                    V.tensor_copy(xrow[:, :, :].bitcast(i32)[:, :, META // 2:META // 2 + 1], tid[:, :].unsqueeze(2))
                    after(g, a)
                    V.tensor_scalar(idx[:, :, :], slotk[:, :, :], float(NS), None, ALU.add).then_inc(idx_ready, 1)
                    a = done(V.tensor_scalar(tid[:, :], tid[:, :], float(GIMG * L), None, ALU.add))

                norm(0, 0, 0)

                def body(it):
                    pairs, groups = not first(it, NIT - 1), not first(it)
                    g = it - 1
                    sums = [window(g, s) for s in range(NSL)]

                    def part(s, n):
                        for _ in range(n):
                            next(sums[s])

                    beside = {
                        (0, 1): lambda: softmax_top(g),
                        (0, 2): lambda: (softmax_end(g), part(0, 6)),
                        (0, 3): lambda: part(0, 12),
                        (1, 0): lambda: (slice_stats(g, 0), part(1, 6)),
                        (1, 1): lambda: part(1, 6),
                        (1, 2): lambda: (part(1, 6), slice_stats(g, 1)),
                        (1, 3): lambda: part(2, 9),
                        (2, 0): lambda: part(2, 5),
                        (2, 1): lambda: (part(2, 4), slice_stats(g, 2)),
                        (3, 2): lambda: (top_two(g), places(g)),
                    } if groups else {}
                    for q in range(PPI):
                        p, j, u = PPI * it + q, 2 * it + q // 2, q % 2
                        for t in range(4):
                            if (q, t) in beside:
                                beside[q, t]()
                            if t == 0 and pairs and not last_pair(it, q):
                                norm(p + 1, j + u, 1 - u)
                            if t < 3 and pairs:
                                attend(p, u, t)
                    if groups and not per_group:
                        per_group.append(counted[0])
                for it in range(2):
                    body(it)
                with dve.Fori(2, NIT - 2) as it:
                    body(it)
                body(NG - 1)
                body(NIT - 1)

            @block.tensor
            def _(pe):
                T_ = nc.tensor

                def patch(p, j, u):
                    pe.wait_ge(x_loaded[u], 16 * (j + 1))
                    for c in range(2):
                        wait(pe, h_in_rows, 2 * p + c - 1)
                        for m in range(2):
                            for kc in range(KC):
                                mm = T_.matmul(bankH[c][:, m * D:(m + 1) * D],
                                               xb[u][:, m, kc * TI + c * 128:kc * TI + c * 128 + 128],
                                               wp_sb[:, kc, :], start=(kc == 0), stop=(kc == KC - 1))
                        mm.then_inc(h_ready, 1)

                def transposes(p, u):
                    pe.wait_ge(qn_ready, p + 1)
                    for t in range(3):
                        wait(pe, qT_done, 3 * p + t - 1)
                        for c in range(3):
                            T = CT[c]
                            mm = T_.transpose(bankT[(u + t) % 2][:, c * 128:c * 128 + T],
                                              qn[u][0:T, c, TILE_AT[t]:TILE_AT[t] + 128], idn[0:T, 0:T])
                        mm.then_inc(tq_ready, 1)

                def conv(p, u, t):
                    pe.wait_ge(qT_done, 3 * p + t + 1)
                    wait(pe, ca_done, 3 * p + t - 1)
                    for k in range(K):
                        mm = T_.matmul(bankK[(u + t) % 2][:, 0:L], conv_w[:, t // 2, k, :],
                                       qT[u][:, t, k:k + L], start=(k == 0), stop=(k == K - 1))
                    mm.then_inc(key_ready, 1)

                def values(p, u, c):
                    pe.wait_ge(qT_done, 3 * p + 3)
                    wait(pe, v_evac, 3 * p + c)
                    T, lo = CT[c], PAD + 128 * c
                    T_.matmul(bankV[0:T, 0:D], qT[u][:, 0, lo:lo + T], ptA_sb[:, :], start=True, stop=False)
                    T_.matmul(bankV[0:T, D:2 * D], qT[u][:, 1, lo:lo + T], ptA_sb[:, :], start=False, stop=False)
                    T_.matmul(bankV[0:T, 0:2 * D], qT[u][:, 2, lo:lo + T], ptB_sb[:, :], start=False, stop=True)\
                      .then_inc(v_ready, 1)

                def scores(p, u, c):
                    pe.wait_ge(ca_done, 3 * p + 3)
                    wait(pe, kern_evac, 3 * p + c)
                    T, n = CT[c], HA * K
                    for t in range(3):
                        mm = T_.matmul(bankN[0:T, t * n:(t + 1) * n], ca[u][:, t, 128 * c:128 * c + T],
                                       (akB_sb if t == 2 else akA_sb)[:, :], start=True, stop=True)
                    mm.then_inc(kern_ready, 1)

                def logits(g, p):
                    pe.wait_ge(qT_done, 3 * p + 3)
                    pe.wait_ge(kern_evac, 3 * p)
                    for n, r in enumerate(PAIRS):
                        pe.wait_ge(xn_ready, NSL * g + (r + 1) // SL + 1)
                        if n > 1:
                            pe.wait_ge(tr_evac, NQ * g + n - 1)
                        for i in range(3):
                            mm = T_.transpose(bankT[n % 2][:, i * 128:(i + 1) * 128],
                                              hg[:, r:r + 2, :].rearrange("p r d -> p (r d)")[:, i * 128:(i + 1) * 128],
                                              idn[:, :])
                        mm.then_inc(tr_ready, 1)
                        if n:
                            route(g, n - 1)
                    route(g, NQ - 1).then_inc(lg_ready, 1)

                def route(g, n):
                    r = PAIRS[n]
                    pe.wait_ge(tr_evac, NQ * g + n + 1)
                    for i, w in ((0, wgA), (1, wgC)):
                        T_.matmul(bankN[:, (r + i) * E:(r + i + 1) * E], xTr[n % 2][:, i * 256:i * 256 + 128], w[:, :],
                                  start=(i == 0), stop=False)
                    mm = T_.matmul(bankN[:, r * E:(r + 2) * E], xTr[n % 2][:, 128:256], wgP[:, :], start=False, stop=True)
                    if n < NQ - 1:
                        mm.then_inc(routed, 1)
                    return mm

                def counts_before(g, p, c):
                    pe.wait_ge(cnt_ready, g + 1)
                    pe.wait_ge(v_evac, 3 * p + c)
                    T_.matmul(bankV[:, 0:16], low_sb[:, :], cnt[:, :], start=True, stop=True)
                    T_.matmul(bankV[:, 16:32], ones[:, 0:128], cnt[:, :], start=True, stop=True).then_inc(pre_ready, 1)

                pe.wait_ge(const_loaded, NCONST)
                pe.wait_ge(zeroed, 1)
                patch(0, 0, 0)
                transposes(0, 0)

                def body(it):
                    pairs, groups = not first(it, NIT - 1), not first(it)
                    if not pairs:
                        logits(it - 1, 2 * NPAIR // 2 - 1)
                        counts_before(it - 1, NPAIR, 0)
                        return
                    for q in range(PPI):
                        p, j, u = PPI * it + q, 2 * it + q // 2, q % 2
                        routing = q == 3 and groups
                        if not last_pair(it, q):
                            patch(p + 1, j + u, 1 - u)
                        if first(it) and q == 0:
                            pe.wait_ge(conv_w_ready, 1)
                        conv(p, u, 0)
                        values(p, u, 0)
                        conv(p, u, 1)
                        values(p, u, 1)
                        if routing:
                            logits(it - 1, p)
                        conv(p, u, 2)
                        if routing:
                            counts_before(it - 1, p, 2)
                            pe.wait_ge(pre_read, it)
                        values(p, u, 2)
                        if not last_pair(it, q):
                            transposes(p + 1, 1 - u)
                        if routing:
                            pe.wait_ge(lg_read, it)
                        for c in range(3):
                            scores(p, u, c)
                for it in range(2):
                    body(it)
                with pe.Fori(2, NIT - 2) as it:
                    body(it)
                body(NG - 1)
                body(NIT - 1)

        st = ExitStack()
        with st:
            sb, pb, sem = allocator(st)
            NJ, NCH = HID // 128, SLOT_TILE // CHUNK
            NG2 = -(-NCH // 2)
            F1 = 2 * HID
            wstage = sb("wstage", [128, 2 * F1 + NJ * D])
            wh = [sb(f"w_high{n}", [128, 2 * F1 + NJ * D], fp16) for n in range(2)]
            wl = [sb(f"w_low{n}", [128, 2 * F1 + NJ * D], fp16) for n in range(2)]
            NMETA = 5
            xin = [sb(f"xin{n}", [CHUNK, NCH, XW], u16) for n in range(2)]
            meta = [sb(f"meta{n}", [CHUNK, NCH, 4], i32) for n in range(NMETA)]
            wsl = [sb(f"slot_weight{n}", [CHUNK, NCH]) for n in range(NMETA)]
            xT = [sb(f"xeT{n}", [128, 3 * SLOT_TILE], fp16) for n in range(2)]
            sg = [sb(f"silu{n}", [128, HALF]) for n in range(2)]
            hf = [sb(f"hidden32_{n}", [128, SLOT_TILE]) for n in range(2)]
            hh = [sb(f"hidden_high{n}", [128, NJ, SLOT_TILE], fp16) for n in range(2)]
            hl = [sb(f"hidden_low{n}", [128, NJ, SLOT_TILE], fp16) for n in range(2)]
            yb = [sb(f"yb{n}", [CHUNK, NCH, D]) for n in range(2)]
            BX = 1024
            bankX = [pb("bankX0", fp16), pb("bankX1", fp16)]
            bankU = [pb(f"bankU{n}") for n in range(2)]
            bankG = [pb(f"bankG{n}") for n in range(2)]
            bankY = [pb(f"bankY{n}") for n in range(2)]

            w_loaded, w_high, w_low = sem("w_loaded"), sem("w_high_done"), sem("w_low_done")
            xin_loaded = [sem(f"xin_loaded{n}") for n in range(2)]
            added = [sem(f"added{n}") for n in range(2)]
            meta_done = sem("meta_done")
            xt_ready, x0_evac, x1_evac = sem("xt_ready"), sem("x0_evac"), sem("x1_evac")
            up_ready, gate_ready = sem("up_ready"), sem("gate_ready")
            silu_done, prod_done, hi_done, lo_done = sem("silu_done"), sem("prod_done"), sem("hi_done"), sem("lo_done")
            y_ready, y_evac = sem("y_ready"), sem("y_evac")
            block = st.enter_context(nc.Block())
            BODY = 2 * TPE
            NT = E * TPE
            NU = 2 * NJ
            LASTB = E // 2 - 1

            def is_last(i):
                return isinstance(i, int) and i == LASTB

            def loop(eng, body):
                body(0)
                with eng.Fori(1, LASTB) as i:
                    body(i)
                body(LASTB)

            def adds(v, i, t):
                return 16 * NCH * (BODY // 2 * i + (t + 1 - v) // 2)

            @block.sync
            def _(sp):
                def load_w(e):
                    for dst, src in ((wstage[:, 0:F1], W1[bass.ds(e, 1), 0:128, :].rearrange("e p f -> p (e f)")),
                                     (wstage[0:D2, F1:2 * F1], W1[bass.ds(e, 1), 128:D, :].rearrange("e p f -> p (e f)")),
                                     (wstage[D2:128, F1:2 * F1], W1[bass.ds(e, 1), 128:D, :].rearrange("e p f -> p (e f)")),
                                     (wstage[:, 2 * F1:].rearrange("p (j d) -> p j d", d=D),
                                      W2[bass.ds(e, 1), :, :].rearrange("e (j p) d -> p (e j) d", p=128))):
                        sp.dma_start(dst, src).then_inc(w_loaded, 16)

                def body(i):
                    for t in range(BODY):
                        n, ee = BODY * i + t, t // TPE
                        wait(sp, xt_ready, n - 1)
                        wait(sp, meta_done, n - 1)
                        sp.dma_start(xin[t % 2][:, :, :], xslots[bass.ds(n * SLOT_TILE, SLOT_TILE), :]
                                     .rearrange("(p j) f -> p j f", j=NCH)).then_inc(xin_loaded[t % 2], 16)
                        if t % TPE == 1 and not (is_last(i) and ee == 1):
                            e = 2 * i + ee + 1
                            wait(sp, w_high, e)
                            wait(sp, w_low, e)
                            load_w(e)
                load_w(0)
                loop(sp, body)

            @block.gpsimd
            def _(pool):
                def body(i):
                    for t in range(BODY):
                        n, v = BODY * i + t, t % 2
                        pool.wait_ge(y_evac, NG2 * (n + 1))
                        if t % TPE == 0:
                            for v2 in range(2):
                                wait(pool, added[v2], adds(v2, i, t))
                        settled(pool)
                        for c in range(NCH):
                            nc.gpsimd.indirect_dma_start(
                                out=out[:, :], out_offset=bass.IndirectOffsetOnAxis(ap=meta[t % NMETA][:, c, 0:1], axis=0),
                                in_=yb[v][:, c, :], in_offset=None, compute_op=ALU.add).then_inc(added[v], 16)
                loop(pool, body)
                for v in range(2):
                    pool.wait_ge(added[v], adds(v, E // 2, 0))

            @block.scalar
            def _(act):
                def split_w(e, ee):
                    act.wait_ge(w_loaded, 64 * (e + 1))
                    nc.scalar.mul(wh[ee][:, :], wstage[:, :], WSCALE).then_inc(w_high, 1)

                def inputs_out(i, t):
                    n, v = BODY * i + t, t % 2
                    act.wait_ge(xt_ready, n + 1)
                    wait(act, up_ready, NU * (n - 1))
                    nc.scalar.copy(xT[v][:, 0:BX], bankX[0][:, :]).then_inc(x0_evac, 1)
                split_w(0, 0)
                inputs_out(0, 0)

                def body(i):
                    for t in range(BODY):
                        n, v, ee = BODY * i + t, t % 2, t // TPE

                        def high(j):
                            act.wait_ge(prod_done, NU * n + 2 * j + 2)
                            if j == 0:
                                wait(act, y_ready, NG2 * (n - 1))
                            nc.scalar.copy(hh[v][:, j, :], hf[j % 2][:, :]).then_inc(hi_done, 1)
                        for j in range(NJ):
                            for m in range(2):
                                w = 2 * j + m
                                act.wait_ge(gate_ready, NU * n + w + 1)
                                wait(act, prod_done, NU * n + w - 1)
                                nc.scalar.activation(sg[m][:, :], bankG[m][:, 0:HALF], ACT.Silu,
                                                     scale=1 / WSCALE).then_inc(silu_done, 1)
                            if j:
                                high(j - 1)
                            if j == 2 and t + 1 < BODY:
                                inputs_out(i, t + 1)
                        high(NJ - 1)
                        if t + 1 == BODY and not is_last(i):
                            inputs_out(i + 1, 0)
                        if t % TPE == 2 and not (is_last(i) and ee == 1):
                            wait(act, y_ready, NG2 * (n - 2))
                            split_w(2 * i + ee + 1, 1 - ee)
                loop(act, body)

            @block.vector
            def _(dve):
                V = nc.vector

                def split_w(e, ee):
                    dve.wait_ge(w_high, e + 1)
                    V.scalar_tensor_tensor(wl[ee][:, :], wstage[:, :], WSCALE, wh[ee][:, :], ALU.mult, ALU.subtract)\
                        .then_inc(w_low, 1)

                def inputs_out(i, t):
                    n, v = BODY * i + t, t % 2
                    dve.wait_ge(xt_ready, n + 1)
                    wait(dve, up_ready, NU * (n - 1))
                    V.tensor_copy(xT[v][:, BX:3 * SLOT_TILE], bankX[1][:, 0:3 * SLOT_TILE - BX]).then_inc(x1_evac, 1)
                split_w(0, 0)
                inputs_out(0, 0)

                def evac_y(i, t, first_t):
                    n, v = BODY * i + t, t % 2
                    wait(dve, added[v], adds(v, i, t))
                    for b in range(NG2):
                        dve.wait_ge(y_ready, NG2 * n + b + 1)
                        for c in range(2 * b, min(2 * b + 2, NCH)):
                            last = V.tensor_scalar(yb[v][:, c, :], bankY[(NG2 * t + b) % 2][:, (c % 2) * D:(c % 2 + 1) * D],
                                                   wsl[t % NMETA][:, c:c + 1], None, ALU.mult)
                        last.then_inc(y_evac, 1)

                def body(i):
                    for t in range(BODY):
                        n, v, ee, te = BODY * i + t, t % 2, t // TPE, t % TPE
                        dve.wait_ge(xin_loaded[v], 16 * (BODY // 2 * i + t // 2 + 1))
                        wait(dve, added[(t - NMETA) % 2], adds((t - NMETA) % 2, i, t - NMETA + 1))
                        xm = xin[v][:, :, :].bitcast(i32)
                        V.tensor_copy(meta[t % NMETA][:, :, :], xm[:, :, META // 2:META // 2 + 4])
                        parts = [(0, CHUNK, int(te > MIX))] if te != MIX else [(0, MIXP, 0), (MIXP, CHUNK, 1)]
                        for lo, hi, k in parts:
                            last = V.tensor_scalar(wsl[t % NMETA][lo:hi, :],
                                                   xin[v][lo:hi, :, :].bitcast(fp32)[:, :, META // 2 + 1 + k],
                                                   WSCALE ** -2, None, ALU.mult)
                        last.then_inc(meta_done, 1)

                        def low(j):
                            dve.wait_ge(hi_done, NJ * n + j + 1)
                            V.tensor_tensor(hl[v][:, j, :], hf[j % 2][:, :], hh[v][:, j, :], ALU.subtract)\
                                .then_inc(lo_done, 1)
                        for j in range(NJ):
                            for m in range(2):
                                w = 2 * j + m
                                dve.wait_ge(silu_done, NU * n + w + 1)
                                dve.wait_ge(up_ready, NU * n + w + 1)
                                if m == 0:
                                    wait(dve, lo_done, NJ * n + j - 1)
                                V.tensor_tensor(hf[j % 2][:, m * HALF:(m + 1) * HALF], sg[m][:, :],
                                                bankU[m][:, 0:HALF], ALU.mult).then_inc(prod_done, 1)
                            if j:
                                low(j - 1)
                            if j == 2 and t + 1 < BODY:
                                inputs_out(i, t + 1)
                        low(NJ - 1)
                        if t + 1 == BODY and not is_last(i):
                            inputs_out(i + 1, 0)
                        if t:
                            evac_y(i, t - 1, t)
                        if t % TPE == 2 and not (is_last(i) and ee == 1):
                            split_w(2 * i + ee + 1, 1 - ee)
                    evac_y(i, BODY - 1, BODY)
                loop(dve, body)

            @block.tensor
            def _(pe):
                T_ = nc.tensor

                def tr(i, t):
                    n, v = BODY * i + t, t % 2
                    pe.wait_ge(xin_loaded[v], 16 * (BODY // 2 * i + t // 2 + 1))
                    wait(pe, x0_evac, n)
                    wait(pe, x1_evac, n)
                    for c in range(NCH):
                        for at, ch in ((0, 0), (SLOT_TILE, 128), (2 * SLOT_TILE, LOA)):
                            b, col = divmod(at + c * CHUNK, BX)
                            mm = T_.transpose(bankX[b][:, col:col + CHUNK], xin[v][:, c, ch:ch + 128].bitcast(fp16),
                                              idn16[:, :])
                    mm.then_inc(xt_ready, 1)

                def up(i, t):
                    n, v, ee = BODY * i + t, t % 2, t // TPE
                    if t % TPE == 0:
                        pe.wait_ge(w_high, 2 * i + ee + 1)
                        pe.wait_ge(w_low, 2 * i + ee + 1)
                    pe.wait_ge(x0_evac, n + 1)
                    pe.wait_ge(x1_evac, n + 1)
                    for j in range(NJ):
                        for m in range(2):
                            high, both, low = (xT[v][:, q * SLOT_TILE + m * HALF:q * SLOT_TILE + (m + 1) * HALF] for q in range(3))
                            for half, bank, ready, free in ((1, bankG, gate_ready, silu_done), (0, bankU, up_ready, prod_done)):
                                wait(pe, free, NU * n + 2 * j + m - 1)
                                lo = half * HID + j * 128
                                o = bank[m][:, 0:HALF]
                                T_.matmul(o, wh[ee][:, lo:lo + 128], high, start=True, stop=False)
                                T_.matmul(o, wh[ee][:, lo:lo + 128], low, start=False, stop=False)
                                T_.matmul(o, wl[ee][:, lo:lo + 128], high, start=False, stop=False)
                                T_.matmul(o, wh[ee][:, F1 + lo:F1 + lo + 128], both, start=False, stop=False)
                                T_.matmul(o, wl[ee][:, F1 + lo:F1 + lo + 128], both, start=False, stop=True)\
                                  .then_inc(ready, 1)

                def down(i, t):
                    n, v, ee = BODY * i + t, t % 2, t // TPE
                    pe.wait_ge(lo_done, NJ * n + NJ)
                    for b in range(NG2):
                        wait(pe, y_evac, NG2 * n + b - 1)
                        for c in range(2 * b, min(2 * b + 2, NCH)):
                            cs = slice(c * CHUNK, (c + 1) * CHUNK)
                            o = bankY[(NG2 * t + b) % 2][:, (c % 2) * D:(c % 2 + 1) * D]
                            for j in range(NJ):
                                ws = slice(2 * F1 + j * D, 2 * F1 + (j + 1) * D)
                                T_.matmul(o, hh[v][:, j, cs], wh[ee][:, ws], start=(j == 0), stop=False)
                                T_.matmul(o, hh[v][:, j, cs], wl[ee][:, ws], start=False, stop=False)
                                mm = T_.matmul(o, hl[v][:, j, cs], wh[ee][:, ws], start=False, stop=(j == NJ - 1))
                        mm.then_inc(y_ready, 1)

                tr(0, 0)

                def body(i):
                    for t in range(BODY):
                        if t + 1 < BODY:
                            tr(i, t + 1)
                        elif not is_last(i):
                            tr(i + 1, 0)
                        up(i, t)
                        if t:
                            down(i, t - 1)
                    down(i, BODY - 1)
                loop(pe, body)


def _hilbert():
    pts = []
    for d in range(TI):
        t, x, y, s = d, 0, 0, 1
        while s < CURVE:
            rx = 1 & t // 2
            ry = 1 & (t ^ rx)
            if ry == 0:
                if rx == 1:
                    x, y = s - 1 - x, s - 1 - y
                x, y = y, x
            x, y, t, s = x + s * rx, y + s * ry, t // 4, s * 2
        pts.append((min(x, GRID - 1), min(y, GRID - 1)))
    return np.array(pts)


def _layout(a):
    f = np.float32
    pts = _hilbert()
    xs = np.asarray(a["x"]).reshape(B, CIN, GRID, PATCH, GRID, PATCH)
    xs = xs[:, :, pts[:, 0], :, pts[:, 1], :]
    xs = xs.transpose(1, 2, 3, 4, 0).reshape(B, KC, 128, TI).transpose(0, 2, 1, 3).reshape(B, 128, KC * TI)
    wt = np.asarray(a["L0_tok_W"]).reshape(D, KC, 128).transpose(2, 1, 0)
    dwt = np.asarray(a["L0_attn_dw_w"]).reshape(D, K)
    dwl = np.stack([dwt[:128], np.concatenate([dwt[128:], dwt[128:]])], 1)
    pww, akw = np.asarray(a["L0_attn_pw_w"]), np.asarray(a["L0_attn_ak_w"])
    heads = [list(range(HA)), list(range(HA, H)) * 2]
    pwl = np.zeros((128, 2, 128), f)
    akl = [np.zeros((128, HA * K), f), np.zeros((128, HA * K), f)]
    for t in range(2):
        for n, h in enumerate(heads[t]):
            pwl[n * IPG:(n + 1) * IPG, t, n * IPG:(n + 1) * IPG] = pww[h].T
            akl[t][n * IPG:(n + 1) * IPG, n * K:(n + 1) * K] = akw[h].T
    pb = np.asarray(a["L0_attn_pw_b"])
    pwbl = np.stack([pb[:128], np.concatenate([pb[128:], pb[128:]])], 1)
    ptt = np.asarray(a["L0_attn_pt_w"]).T
    ptBl = np.zeros((128, 2 * D), f)
    ptBl[:D2, :D] = ptt[128:]
    ptBl[D2:, D:] = ptt[128:]

    def rep(v, n=1):
        return np.broadcast_to(np.tile(np.asarray(v), n), (128, n * len(v)))
    wgate = np.asarray(a["L0_ffn_Wg"])
    wgpair = np.zeros((128, 2 * E), f)
    wgpair[:D2, :E] = wgate[128:]
    wgpair[D2:, E:] = wgate[:D2]
    revrank = np.broadcast_to(np.tile(E - np.arange(E), R), (128, R * E)).astype(f)
    valid = np.array([[(p % SEG) * R + r < L for r in range(R)] for p in range(128)]).astype(f)
    tokid = np.array([[(p // SEG) * L + (p % SEG) * R + r for r in range(R)] for p in range(128)]).astype(f)
    slotbase = np.broadcast_to(np.array([e * CAPE + k * CAPK - 1 for k in range(TOPK) for e in range(E)]), (128, 16))
    return {
        "x": xs, "txt": np.asarray(a["txt"]), "wpatch": wt, "tokb": rep(a["L0_tok_b"], 2), "dw": dwl, "pw": pwl,
        "pwb": pwbl, "akA": akl[0], "akB": akl[1], "akb": rep(a["L0_attn_ak_b"]), "ptA": ptt[:128], "ptB": ptBl,
        "ptb": rep(a["L0_attn_pt_b"], 2), "wg": wgate, "wgpair": wgpair, "W1": np.asarray(a["L0_ffn_W1"]),
        "W2": np.asarray(a["L0_ffn_W2"]), "ident": np.eye(128, dtype=f),
        "lower": np.triu(np.ones((128, 128), f), 1), "revrank": revrank, "valid": valid,
        "slotbase": slotbase.astype(f), "tokid": tokid,
    }


def kernel(**inputs):
    import concourse.bacc as _bacc
    from concourse.bass_utils import run_bass_kernel_spmd as _run

    nc = _bacc.Bacc("TRN2", target_bir_lowering=False, num_devices=1)
    arrays, args = {}, {}
    for name, a in _layout(inputs).items():
        a = np.ascontiguousarray(a)
        arrays[f"in_{name}"] = a
        args[name] = nc.dram_tensor(f"in_{name}", a.shape, mybir.dt.from_np(a.dtype), kind="ExternalInput").ap()
    args["out"] = nc.dram_tensor("out_0", (N + 2 * SLOT_TILE, D), mybir.dt.float32, kind="ExternalOutput").ap()
    build(nc, **args)
    r = _run(nc, [arrays], core_ids=[0])
    return r.results[0]["out_0"][:N].reshape(B, L, D)
```

```python
import numpy as np
import concourse.bass as bass
from concourse import mybir
from contextlib import ExitStack

B, CIN, IMG, PATCH = 32, 3, 224, 16
GRID = IMG // PATCH
CURVE = 16
TI, TT, D = CURVE * CURVE, 77, 192
L = TI + TT
KC = CIN * PATCH * PATCH // 128
H, IPG, K = 12, 16, 9
PAD = (K - 1) // 2
D2 = D - 128
HA = 128 // IPG
HB = H - HA
E, TOPK, HID = 8, 2, 512
CAP = int(1.2 * B * L / E)
SLOT_TILE, CHUNK = 640, 128
HALF = SLOT_TILE // 2
TPE = -(-TOPK * CAP // SLOT_TILE)
CAPE = TPE * SLOT_TILE
CAPK = CAPE // TOPK
MIX, MIXP = CAPK // SLOT_TILE, CAPK % SLOT_TILE * CHUNK // SLOT_TILE
NS = E * CAPE
N = B * L
EPS = 1e-5

NPAIR = B // 2
CT = [128, 128, TT]
ROW = 2 * D + H * K
SEG, R = 16, 21
LROWS = SEG * R + 2 * PAD
GIMG = 128 // SEG
NG = B // GIMG
RL = L - (SEG - 1) * R
SLICES = [(0, 8), (8, 16), (16, R)]
NSL = len(SLICES)
WIDE = max(b - a for a, b in SLICES)
LOWN = SLICES[-1][1] - SLICES[-1][0]
BIG = 1e30
NIT = NG + 1
LOB, LOA, META = D, D + D2, 2 * D
XW = META + 8
WSCALE = 64.0


def build(nc, x, txt, wpatch, tokb, dw, pw, pwb, akA, akB, akb, ptA, ptB, ptb, wg, wgpair, W1, W2,
          ident, lower, revrank, valid, slotbase, tokid, out):
    fp32, fp16, i32, u16 = mybir.dt.float32, mybir.dt.float16, mybir.dt.int32, mybir.dt.uint16
    ALU, ACT, AX = mybir.AluOpType, mybir.ActivationFunctionType, mybir.AxisListType

    rows = nc.dram_tensor("token_rows", (B, LROWS, ROW), fp32, kind="Internal").ap()
    xslots = nc.dram_tensor("expert_inputs", (NS, XW), u16, kind="Internal").ap()

    def wait(eng, sem, value):
        if isinstance(value, int) and value <= 0:
            return
        eng.wait_ge(sem, value)

    def settled(eng):
        eng.sem_inc(passed, 1)

    top = ExitStack()
    with top:
        def allocator(stack):
            return (lambda n, s, dt=fp32: stack.enter_context(nc.sbuf_tensor(n, s, dt)),
                    lambda n, dt=fp32: stack.enter_context(nc.psum_tensor(n, [128, 2048 // (4 if dt == fp32 else 2)], dt)),
                    lambda n: stack.enter_context(nc.semaphore(n)))
        sb, _, sem = allocator(top)
        passed = sem("passed")

        idn16 = sb("identity16", [128, 128], fp16)
        xrow = sb("slot_rows", [128, R, XW], u16)
        xrow16 = xrow[:, :, :].bitcast(fp16)
        idx = sb("slots", [128, TOPK, R], i32)

        def scatter_rows(n, done):
            k, r = n // R, n % R
            nc.gpsimd.indirect_dma_start(
                out=xslots[:, :], out_offset=bass.IndirectOffsetOnAxis(ap=idx[:, k, r:r + 1], axis=0),
                in_=xrow[:, r, :], in_offset=None, bounds_check=NS - 1, oob_is_err=False).then_inc(done, 16)

        st = ExitStack()
        with st:
            sb, pb, sem = allocator(st)
            idn = sb("identity", [128, 128])
            wp_sb = sb("wp_sb", [128, KC, D])
            tokb_sb = sb("tokb_sb", [128, 2 * D])
            dw_sb = sb("dw_sb", [128, 2, K])
            pw_sb = sb("pw_sb", [128, 2, 128])
            pwb_sb = sb("pwb_sb", [128, 2])
            akA_sb = sb("akA_sb", [128, HA * K])
            akB_sb = sb("akB_sb", [128, 2 * HB * K])
            ptA_sb = sb("ptA_sb", [128, D])
            ptB_sb = sb("ptB_sb", [128, 2 * D])
            ptb_sb = sb("ptb_sb", [128, 2 * D])
            conv_w = sb("conv_w", [128, 2, K, 128])
            xb = [sb(f"patches{u}", [128, 2, KC * TI]) for u in range(2)]
            rowb = [sb(f"rowbuf{u}", [128, 3, 2, ROW]) for u in range(2)]
            qn = [sb(f"normed{u}", [128, 3, 2 * D]) for u in range(2)]
            TILE_AT = [0, 2 * 128, 128]
            qT = [sb(f"normedT{u}", [128, 3, L + 2 * PAD]) for u in range(2)]
            ca = [sb(f"conv_attn{u}", [128, 3, L]) for u in range(2)]
            stats = sb("stats", [128, 6, 6])
            mv = sb("mean_var", [128, 6, 2])
            rs = sb("rstd", [128, 2, 6])
            tmp6 = sb("tmp6", [128, 2, 6])
            cst = sb("pool_constants", [128, 3, R])
            zeros = sb("zeros", [128, ROW])
            empty = [sb(f"empty_slots{v}", [CHUNK, SLOT_TILE // CHUNK, XW], u16) for v in range(2)]

            vx = sb("window_values", [128, (R + 2 * PAD) * D])
            kb = sb("kb", [128, R * H, K])
            hg = sb("hidden_group", [128, R, D])
            akb_sb = sb("akb_sb", [128, H * K])
            kmax = sb("kmax", [128, R * H])
            ksum = sb("ksum", [128, R * H])
            krec = sb("krec", [128, R * H])
            prod = [sb(f"prod{n}", [128, WIDE * D]) for n in range(2)]
            prodP = [empty[v][:, :, :].rearrange("p j f -> p (j f)").bitcast(fp32)[:, 0:LOWN * D] for v in range(2)]
            stats2 = sb("stats2", [128, R, 6])
            mv2 = sb("mean_var2", [128, R, 2])
            rs2 = sb("rstd2", [128, 2, R])
            tmp21 = sb("tmp21", [128, 2, R])
            xTr = [sb(f"xTr{n}", [128, 3 * 128]) for n in range(2)]
            wgA, wgP, wgC = sb("wgA", [128, E]), sb("wgP", [128, 2 * E]), sb("wgC", [128, E])
            low_sb, ones = sb("lower_sb", [128, 128]), sb("ones", [128, TOPK * E * R])
            rev, val, tid = sb("rev", [128, R * E]), sb("val", [128, R]), sb("token_numbers", [128, R])
            sbase = sb("sbase", [128, TOPK * E])
            lg, lg2, eq = sb("lg", [128, R, E]), sb("lg2", [128, R, E]), sb("eq", [128, R, E])
            m12, i12 = sb("m12", [128, TOPK, R]), sb("i12", [128, TOPK, R])
            oh = sb("onehot", [128, TOPK * E, R])
            ohv = sb("onehot_valid", [128, TOPK * E, R])
            inc = sb("running_count", [128, TOPK * E * R])
            cnt, off, base = sb("cnt", [128, 16]), sb("off", [128, 16]), sb("base", [128, 16])
            pos, pos2 = sb("pos", [128, TOPK * E, R]), sb("pos2", [128, TOPK * E, R])
            posk, slotk = sb("posk", [128, TOPK, R]), sb("slotk", [128, TOPK, R])
            keep = sb("keep", [128, TOPK, R])
            gap, ex, w12 = sb("gap", [128, R]), sb("ex", [128, R]), sb("w12", [128, TOPK, R])

            bankH = [pb(f"bankH{c}") for c in range(2)]
            bankT = [pb(f"bankT{c}") for c in range(2)]
            bankK = [pb(f"bankK{c}") for c in range(2)]
            bankL = [bankK[0], bankK[1], bankH[0]]
            prodL = [xb[u][:, 0, 0:SLICES[0][1] * D] for u in range(2)]
            bankV = pb("bankV")
            bankN = pb("bankN")

            first_loaded = sem("first_loaded")
            const_loaded = sem("const_loaded")
            zeroed = sem("zeroed")
            empty_set = sem("empty_set")
            margins_done = sem("margins_done")
            fill_done = sem("fill_done")
            x_loaded = [sem(f"x_loaded{u}") for u in range(2)]
            txt_loaded = [sem(f"txt_loaded{u}") for u in range(2)]
            row_stored = [sem(f"row_stored{u}") for u in range(2)]
            conv_w_ready = sem("conv_w_ready")
            h_ready = sem("h_ready")
            h_in_rows = sem("h_in_rows")
            stats_done = sem("stats_done")
            aggr_done = sem("aggr_done")
            pool_step = sem("pool_step")
            pool_step2 = sem("pool_step2")
            cst_set = sem("cst_set")
            qn_ready = sem("qn_ready")
            tq_ready = sem("tq_ready")
            qT_done = sem("qT_done")
            key_ready = sem("key_ready")
            ca_done = sem("ca_done")
            v_ready = sem("v_ready")
            v_evac = sem("v_evac")
            kern_ready = sem("kern_ready")
            kern_evac = sem("kern_evac")

            vk_loaded = sem("vk_loaded")
            hg_loaded = sem("hg_loaded")
            step = sem("vector_step")
            sc_ready, sc_exp = sem("sc_ready"), sem("sc_exp")
            weights_done = sem("weights_done")
            tap_made, tap_summed = sem("tap_made"), sem("tap_summed")
            sum_out = sem("sum_out")
            pool_sum = sem("pool_sum")
            window_done = sem("window_done")
            aggr2_done = sem("aggr2_done")
            xn_ready, xh_ready, xl_ready = sem("xn_ready"), sem("xh_ready"), sem("xl_ready")
            tr_ready, tr_evac, lg_ready, lg_read = sem("tr_ready"), sem("tr_evac"), sem("lg_ready"), sem("lg_read")
            routed = sem("routed")
            gap_ready, ex_ready = sem("gap_ready"), sem("ex_ready")
            cnt_ready, pre_ready, pre_read = sem("cnt_ready"), sem("pre_ready"), sem("pre_read")
            idx_ready, scattered, rows_sent = sem("idx_ready"), sem("scattered"), sem("rows_sent")
            h_stored = [sem(f"h_stored{s}") for s in range(NSL)]

            block = st.enter_context(nc.Block())

            CONSTS = [(idn[:, :], ident), (wp_sb[:, :, :], wpatch), (tokb_sb[:, :], tokb), (dw_sb[:, :, :], dw),
                      (pw_sb[:, :, :], pw), (pwb_sb[:, :], pwb), (akA_sb[:, :], akA), (akB_sb[:, :], akB),
                      (ptA_sb[:, :], ptA), (ptB_sb[:, :], ptB), (ptb_sb[:, :], ptb),
                      (akb_sb[:, :], akb), (wgA[:, :], wg[0:128, :]), (wgP[:, :], wgpair), (wgC[:, :], wg[D2:D, :]), (low_sb[:, :], lower),
                      (rev[:, :], revrank), (val[:, :], valid), (sbase[:, :], slotbase), (tid[:, :], tokid)]
            NFIRST = 3
            NCONST = 16 * (len(CONSTS) - NFIRST)
            NFILL = 2 * E
            NPOOL = 4
            PAIRS = [min(2 * n, R - 2) for n in range(-(-R // 2))]
            NQ = len(PAIRS)
            hgf = hg[:, :, :].rearrange("p r d -> p (r d)")
            LCOLS = [min(512, SLICES[0][1] * D - b * 512) for b in range(len(bankL))]
            AFTER = [sum(r + 2 <= hi for r in PAIRS) for hi in [0] + [hi for _, hi in SLICES]]
            NST = GIMG + 1
            GI3 = 2 * (GIMG // 2 - 1)
            NSC = TOPK * R
            PPI = GIMG // 2

            def first(it, n=0):
                return isinstance(it, int) and it == n

            def last_pair(it, q):
                return first(it, NG - 1) and q == PPI - 1

            @block.sync
            def _(sp):
                def load_x(j, u):
                    sp.dma_start(xb[u][:, :, :], x[bass.ds(4 * j + 2 * u, 2), :, :].rearrange("b p f -> p b f"))\
                      .then_inc(x_loaded[u], 16)

                def load_txt(j, u):
                    wait(sp, row_stored[u], 64 * j)
                    sp.dma_start(rowb[u][0:TT, 2, :, D:2 * D],
                                 txt[bass.ds(4 * j + 2 * u, 2), :, :].rearrange("b t d -> t b d"))\
                      .then_inc(txt_loaded[u], 16)

                def store(j, u):
                    p = 2 * j + u
                    sp.wait_ge(v_evac, 3 * p + 3)
                    sp.wait_ge(kern_evac, 3 * p + 3)
                    for m in range(2):
                        img = rows[bass.ds(2 * p + m, 1), :, :]
                        sp.dma_start(img[:, PAD:PAD + TI, :].rearrange("b (c p) f -> p (b c) f", p=128),
                                     rowb[u][:, 0:2, m, :]).then_inc(row_stored[u], 16)
                        sp.dma_start(img[:, PAD + TI:PAD + L, :].rearrange("b p f -> p (b f)"),
                                     rowb[u][0:TT, 2, m, :]).then_inc(row_stored[u], 16)

                def load_vk(g, lo, hi):
                    sp.wait_ge(row_stored[0], 64 * (2 * g + 2 if hi > 4 else 2 * g + 1))
                    sp.wait_ge(row_stored[1], 64 * (2 * g + 2 if hi > 6 else 2 * g + 1))
                    wait(sp, window_done, NSL * g)
                    for m in range(lo, hi):
                        seg = rows[bass.ds(g * GIMG + m, 1), :, :]
                        ps = slice(m * SEG, (m + 1) * SEG)
                        body = seg[:, PAD:PAD + SEG * R, :].rearrange("b (s r) f -> (b s) r f", r=R)
                        sp.dma_start(kb[ps, :, :].rearrange("p (r h) k -> p r (h k)", h=H),
                                     body[:, :, 2 * D:ROW]).then_inc(vk_loaded, 16)
                        sp.dma_start(vx[ps, 0:R * D].rearrange("p (r d) -> p r d", d=D),
                                     seg[:, 0:SEG * R, 0:D].rearrange("b (s r) f -> (b s) r f", r=R))\
                          .then_inc(vk_loaded, 16)
                        sp.dma_start(vx[ps, R * D:(R + 2 * PAD) * D].rearrange("p (r d) -> p r d", d=D),
                                     seg[:, 2 * PAD:2 * PAD + SEG * R, 0:D]
                                     .rearrange("b (s r) f -> (b s) r f", r=R)[:, R - 2 * PAD:R, :])\
                          .then_inc(vk_loaded, 16)

                def load_hidden(g):
                    wait(sp, tr_ready, NQ * g)
                    wait(sp, xh_ready, NSL * g)
                    wait(sp, xl_ready, NSL * g)
                    for m in range(GIMG):
                        seg = rows[bass.ds(g * GIMG + m, 1), :, :]
                        sp.dma_start(hg[m * SEG:(m + 1) * SEG, :, :],
                                     seg[:, PAD:PAD + SEG * R, D:2 * D].rearrange("b (s r) f -> (b s) r f", r=R))\
                          .then_inc(hg_loaded, 16)

                def store_slice(g, s):
                    sp.wait_ge(window_done, NSL * g + s + 1)
                    full, (lo, hi) = (SEG - 1) * R, SLICES[s]
                    dst = out[bass.ds(g * GIMG * L, GIMG * L), :].rearrange("(m l) d -> m l d", l=L)
                    sp.dma_start(dst[:, full + lo:full + min(hi, RL), :], hg[SEG - 1::SEG, lo:min(hi, RL), :])\
                      .then_inc(h_stored[s], 16)
                    for m in range(GIMG):
                        sp.dma_start(dst[m:m + 1, 0:full, :].rearrange("m (s r) d -> (m s) r d", r=R)[:, lo:hi, :],
                                     hg[m * SEG:(m + 1) * SEG - 1, lo:hi, :]).then_inc(h_stored[s], 16)

                load_x(0, 0)
                for dst, src in CONSTS[:NFIRST]:
                    sp.dma_start(dst, src).then_inc(first_loaded, 16)
                load_x(0, 1)
                sp.wait_ge(zeroed, 1)
                for u in range(2):
                    load_txt(0, u)
                sp.wait_ge(h_ready, 2)
                load_x(1, 0)

                def body(it):
                    pairs, groups = not first(it, NIT - 1), not first(it)
                    for q in range(PPI):
                        if groups and q == 3:
                            store_slice(it - 1, 1)
                            store_slice(it - 1, 2)
                        if pairs:
                            j, u = 2 * it + q // 2, q % 2
                            if not (first(it, NG - 1) and q >= 1):
                                sp.wait_ge(h_ready, 2 * (PPI * it + q + 1) + 2)
                                load_x(j + 1 + u, 1 - u)
                            if q == 3:
                                if first(it):
                                    sp.wait_ge(margins_done, 16 * 3)
                                load_vk(it, 0, GI3)
                        if groups and q == 1:
                            store_slice(it - 1, 0)
                        if pairs:
                            store(j, u)
                            if not (first(it, NG - 1) and q >= 2):
                                load_txt(j + 1, u)
                    if pairs:
                        load_vk(it, GI3, GIMG)
                        load_hidden(it)
                for it in range(2):
                    body(it)
                with sp.Fori(2, NIT - 2) as it:
                    body(it)
                body(NG - 1)
                body(NIT - 1)
                for s in range(NSL):
                    sp.wait_ge(h_stored[s], 16 * NST * NG)

            @block.gpsimd
            def _(pool):
                for k, c in enumerate((-0.5, EPS, -1.0)):
                    nc.gpsimd.memset(cst[:, k, :], c).then_inc(cst_set, 1)
                pool.wait_ge(zeroed, 1)
                for v in range(2):
                    nc.gpsimd.iota(empty[v][:, :, :].bitcast(i32)[:, :, META // 2:META // 2 + 1],
                                   [[1, SLOT_TILE // CHUNK]], base=N + v * SLOT_TILE,
                                   channel_multiplier=SLOT_TILE // CHUNK).then_inc(empty_set, 1)
                pool.wait_ge(cst_set, 3)

                def layer_norm(mean, var, tmp, res, n, sem_, at):
                    TTn = nc.gpsimd.tensor_tensor
                    TTn(tmp[:, 0, :], var, cst[:, 1, 0:n], ALU.add).then_inc(sem_, 1)
                    pool.wait_ge(sem_, at + 1)
                    TTn(res[:, 0, :], tmp[:, 0, :], cst[:, 0, 0:n], ALU.pow).then_inc(sem_, 1)
                    pool.wait_ge(sem_, at + 2)
                    TTn(tmp[:, 1, :], mean, res[:, 0, :], ALU.mult).then_inc(sem_, 1)
                    pool.wait_ge(sem_, at + 3)
                    TTn(res[:, 1, :], tmp[:, 1, :], cst[:, 2, 0:n], ALU.mult).then_inc(sem_, 1)

                def pair_norm(p):
                    pool.wait_ge(aggr_done, p + 1)
                    wait(pool, qn_ready, p)
                    layer_norm(mv[:, :, 0], mv[:, :, 1], tmp6, rs, 6, pool_step, NPOOL * p)

                def group_norm(g, s):
                    ss, n = slice(*SLICES[s]), SLICES[s][1] - SLICES[s][0]
                    pool.wait_ge(aggr2_done, NSL * g + s + 1)
                    layer_norm(mv2[:, ss, 0], mv2[:, ss, 1], tmp21[:, :, ss], rs2[:, :, ss], n, pool_step2,
                               NPOOL * (NSL * g + s))

                def low_parts(g, s):
                    ss = slice(*SLICES[s])
                    pool.wait_ge(xh_ready, NSL * g + s + 1)
                    nc.gpsimd.tensor_tensor(xrow16[:, ss, LOB:LOA], hg[:, ss, 128:D], xrow16[:, ss, 128:D], ALU.subtract)
                    nc.gpsimd.tensor_tensor(xrow16[:, ss, LOA:META], hg[:, ss, 0:128], xrow16[:, ss, 0:128], ALU.subtract)\
                        .then_inc(xl_ready, 1)

                def window(g):
                    lo, hi = SLICES[-1]
                    acc = hg[:, lo:hi, :].rearrange("p a d -> p (a d)")
                    at = 2 * K * g

                    def mult(k):
                        if k >= 2:
                            pool.wait_ge(pool_sum, at + 2 * (k - 1) + 1)
                        nc.gpsimd.tensor_tensor(
                            prodP[k % 2].rearrange("p (a d) -> p a d", d=IPG),
                            vx[:, (lo + k) * D:(hi + k) * D].rearrange("p (a d) -> p a d", d=IPG),
                            kb[:, lo * H:hi * H, k:k + 1].to_broadcast([128, (hi - lo) * H, IPG]), ALU.mult)\
                            .then_inc(pool_sum, 1)

                    def add(k):
                        pool.wait_ge(pool_sum, at + 2 * k + (2 if k < K - 1 else 1))
                        nc.gpsimd.tensor_tensor(acc, acc, prodP[k % 2], ALU.add).then_inc(pool_sum, 1)
                    if first(g):
                        pool.wait_ge(fill_done, 16 * NFILL)
                    pool.wait_ge(weights_done, g + 1)
                    mult(0)
                    pool.wait_ge(hg_loaded, 16 * GIMG * (g + 1))
                    yield
                    for k in range(1, K):
                        mult(k)
                        yield
                        add(k - 1)
                        yield
                    add(K - 1)
                    yield

                def scatter(g, part):
                    if part == 0:
                        pool.wait_ge(idx_ready, g + 1)
                        pool.wait_ge(xl_ready, NSL * g + NSL)
                        settled(pool)
                    for n in range(part * NSC // 3, (part + 1) * NSC // 3):
                        scatter_rows(n, scattered)
                    if part == 2:
                        pool.wait_ge(scattered, 16 * NSC * (g + 1))
                        pool.sem_inc(rows_sent, 1)

                pool.sem_inc(rows_sent, 1)
                pair_norm(0)

                def body(it):
                    older = not first(it) and not first(it, 1)
                    groups, g = not first(it), it - 1
                    sums = window(g)

                    def part(n):
                        for _ in range(n):
                            next(sums)
                    for q in range(PPI):
                        if q == 3 and groups:
                            for s in (1, 2):
                                group_norm(g, s)
                        if not first(it, NIT - 1) and not last_pair(it, q):
                            pair_norm(PPI * it + q + 1)
                        if older and q == 0:
                            scatter(it - 2, 0)
                            scatter(it - 2, 1)
                        if older and q == 1:
                            scatter(it - 2, 2)
                        if q == 1 and groups:
                            part(K if first(it, NIT - 1) else 5)
                            group_norm(g, 0)
                        if q == 2 and groups:
                            part(K if first(it, NIT - 1) else 13)
                        if q == 3 and groups:
                            for s in range(NSL):
                                low_parts(g, s)
                for it in range(2):
                    body(it)
                with pool.Fori(2, NIT - 2) as it:
                    body(it)
                body(NG - 1)
                body(NIT - 1)
                pool.wait_ge(idx_ready, NG)

            @block.scalar
            def _(act):
                for dst, src in CONSTS[NFIRST:]:
                    act.dma_start(dst, src).then_inc(const_loaded, 16)
                act.wait_ge(zeroed, 1)
                act.dma_start(rows[:, 0:PAD, :], zeros[0:B, :].unsqueeze(1).to_broadcast([B, PAD, ROW]))\
                   .then_inc(margins_done, 16)
                tail = LROWS - PAD - L
                act.dma_start(rows[:, PAD + L:LROWS, :], zeros[0:B, :].unsqueeze(1).to_broadcast([B, tail, ROW]))\
                   .then_inc(margins_done, 16)
                act.dma_start(out[N:N + 2 * SLOT_TILE, :].rearrange("(p j) d -> p j d", p=CHUNK),
                              zeros[0:CHUNK, 0:D].unsqueeze(1).to_broadcast([CHUNK, 2 * SLOT_TILE // CHUNK, D]))\
                   .then_inc(margins_done, 16)
                tiles = xslots.rearrange("(e t p j) f -> e p t (j f)", t=TPE, p=CHUNK, e=E)

                def fill(q):
                    for e in range(E // PPI * q, E // PPI * (q + 1)):
                        for v in range(2):
                            act.dma_start(tiles[e][:, v::2, :], empty[v][:, :, :].rearrange("p j f -> p (j f)").unsqueeze(1)
                                          .to_broadcast([CHUNK, (TPE + 1 - v) // 2, SLOT_TILE // CHUNK * XW]))\
                               .then_inc(fill_done, 16)

                def normalise(p, u):
                    act.wait_ge(pool_step, NPOOL * (p + 1))
                    wait(act, tq_ready, 3 * p - 3)
                    for c in (0, 1, 2):
                        for m in range(2):
                            parts = [(0, 0, D)] if m == 0 else [(2 * 128, 0, 128), (D, 128, D2)]
                            for to, ch, n in parts:
                                last = nc.scalar.activation(
                                    qn[u][:, c, to:to + n], rowb[u][:, c, m, D + ch:D + ch + n], ACT.Identity,
                                    bias=rs[:, 1, 2 * c + m:2 * c + m + 1], scale=rs[:, 0, 2 * c + m:2 * c + m + 1])
                    last.then_inc(qn_ready, 1)

                def tiles_out(p, u):
                    for t in range(3):
                        act.wait_ge(tq_ready, 3 * p + t + 1)
                        if t == 0:
                            wait(act, ca_done, 3 * p - 3)
                        nc.scalar.copy(qT[u][:, t, PAD:PAD + L], bankT[(u + t) % 2][:, 0:L]).then_inc(qT_done, 1)

                def scores_out(p, j, u):
                    for c in range(3):
                        act.wait_ge(kern_ready, 3 * p + c + 1)
                        if c == 0:
                            wait(act, row_stored[u], 64 * j)
                        T = CT[c]
                        nc.scalar.copy(rowb[u][0:T, c, :, 2 * D:2 * D + HA * K],
                                       bankN[0:T, 0:2 * HA * K].rearrange("p (m k) -> p m k", m=2))
                        nc.scalar.copy(rowb[u][0:T, c, :, 2 * D + HA * K:ROW],
                                       bankN[0:T, 2 * HA * K:2 * H * K].rearrange("p (m k) -> p m k", m=2))\
                          .then_inc(kern_evac, 1)

                def high_parts(g, s):
                    act.wait_ge(xn_ready, NSL * g + s + 1)
                    if s == 0:
                        act.wait_ge(rows_sent, g + 1)
                    ss = slice(*SLICES[s])
                    nc.scalar.copy(xrow16[:, ss, 0:D], hg[:, ss, :]).then_inc(xh_ready, 1)

                def normalise_slice(g, s):
                    act.wait_ge(pool_step2, NPOOL * (NSL * g + s + 1))
                    act.wait_ge(h_stored[s], 16 * NST * (g + 1))
                    for r in range(*SLICES[s]):
                        last = nc.scalar.activation(hg[:, r, :], hg[:, r, :], ACT.Identity,
                                                    bias=rs2[:, 1, r:r + 1], scale=rs2[:, 0, r:r + 1])
                    last.then_inc(xn_ready, 1)

                def routing_out(g, lo, hi):
                    for n in range(lo, hi):
                        act.wait_ge(tr_ready, NQ * g + n + 1)
                        if n == 0:
                            wait(act, lg_ready, g)
                        if n > 1:
                            act.wait_ge(routed, (NQ - 1) * g + n - 1)
                        nc.scalar.copy(xTr[n % 2][:, :], bankT[n % 2][:, 0:384]).then_inc(tr_evac, 1)

                def body(it):
                    pairs, groups = not first(it, NIT - 1), not first(it)
                    for q in range(PPI):
                        p, j, u = PPI * it + q, 2 * it + q // 2, q % 2
                        more = pairs and not last_pair(it, q)
                        if q == 3 and groups:
                            for s in (1, 2):
                                normalise_slice(it - 1, s)
                                if not pairs:
                                    routing_out(it - 1, AFTER[s], AFTER[s + 1])
                            if pairs:
                                routing_out(it - 1, AFTER[1], NQ)
                            for s in (1, 2):
                                high_parts(it - 1, s)
                        if more:
                            normalise(p + 1, 1 - u)
                        if first(it):
                            if q == 0:
                                act.wait_ge(empty_set, 2)
                            fill(q)
                        if q == 0 and groups:
                            act.wait_ge(sc_ready, it)
                            nc.scalar.activation(kb[:, :, :], kb[:, :, :], ACT.Exp).then_inc(sc_exp, 1)
                            if not pairs:
                                act.wait_ge(tap_summed, K)
                                for b, n in enumerate(LCOLS):
                                    last = nc.scalar.copy(hgf[:, b * 512:b * 512 + n], bankL[b][:, 0:n])
                                last.then_inc(sum_out, 1)
                        if more:
                            tiles_out(p + 1, 1 - u)
                        if q == 3 and groups:
                            act.wait_ge(gap_ready, it)
                            nc.scalar.activation(ex[:, :], gap[:, :], ACT.Exp).then_inc(ex_ready, 1)
                        if pairs:
                            scores_out(p, j, u)
                        if groups and q == 1:
                            normalise_slice(it - 1, 0)
                            high_parts(it - 1, 0)
                        if groups and q == 2:
                            routing_out(it - 1, 0, AFTER[1])
                normalise(0, 0)
                tiles_out(0, 0)
                for it in range(2):
                    body(it)
                with act.Fori(2, NIT - 2) as it:
                    body(it)
                body(NG - 1)
                body(NIT - 1)

            @block.vector
            def _(dve):
                V = nc.vector
                for u in range(2):
                    V.memset(qT[u][:, :, :], 0.0)
                    V.memset(rowb[u][:, 2, :, D:2 * D], 0.0)
                V.memset(xrow[:, :, META:XW], 0)
                V.memset(empty[0][:, :, :], 0)
                V.memset(empty[1][:, :, :], 0)
                V.memset(ones[:, :], 1.0)
                V.memset(base[:, :], 0.0)
                V.memset(zeros[:, :], 0.0).then_inc(zeroed, 1)
                def norm(p, j, u):
                    wait(dve, row_stored[u], 64 * j)
                    for c in range(2):
                        dve.wait_ge(h_ready, 2 * p + c + 1)
                        V.tensor_tensor(rowb[u][:, c, :, D:2 * D],
                                        bankH[c][:, 0:2 * D].rearrange("p (m d) -> p m d", m=2),
                                        tokb_sb[:, :].rearrange("p (m d) -> p m d", m=2), ALU.add)\
                            .then_inc(h_in_rows, 1)
                    dve.wait_ge(txt_loaded[u], 16 * (j + 1))
                    dve.wait_ge(h_in_rows, 2 * p + 2)
                    for c in (2, 0, 1):
                        for m in range(2):
                            last = V.bn_stats(stats[:, 2 * c + m, :], rowb[u][:, c, m, D:2 * D])
                    last.then_inc(stats_done, 1)
                    dve.wait_ge(stats_done, p + 1)
                    wait(dve, pool_step, NPOOL * p)
                    settled(dve)
                    for n in range(6):
                        last = V.bn_aggr(mv[:, n, :], stats[:, n, :])
                    last.then_inc(aggr_done, 1)

                def attend(p, u, t):
                    dve.wait_ge(key_ready, 3 * p + t + 1)
                    wait(dve, kern_ready, 3 * p - 3)
                    V.scalar_tensor_tensor(ca[u][:, t, :], bankK[(u + t) % 2][:, 0:L],
                                           pwb_sb[:, t // 2:t // 2 + 1], qT[u][:, t, PAD:PAD + L],
                                           ALU.add, ALU.mult).then_inc(ca_done, 1)
                    T = CT[t]
                    dve.wait_ge(v_ready, 3 * p + t + 1)
                    V.tensor_tensor(rowb[u][0:T, t, :, 0:D],
                                    bankV[0:T, 0:2 * D].rearrange("p (m d) -> p m d", m=2),
                                    ptb_sb[0:T, :].rearrange("p (m d) -> p m d", m=2), ALU.add)\
                        .then_inc(v_evac, 1)

                counted = [0]
                per_group = []

                def done(ins):
                    ins.then_inc(step, 1)
                    counted[0] += 1
                    return counted[0]

                def after(g, k):
                    dve.wait_ge(step, g * per_group[0] + k if per_group else k)

                def softmax_top(g):
                    counted[0] = 0
                    dve.wait_ge(vk_loaded, 16 * 3 * GIMG * (g + 1))
                    kbf = kb[:, :, :].rearrange("p (r h) k -> p r (h k)", h=H)
                    a = done(V.tensor_tensor(kbf, kbf, akb_sb[:, :].unsqueeze(1).to_broadcast([128, R, H * K]), ALU.add))
                    after(g, a)
                    a = done(V.tensor_reduce(kmax[:, :], kb[:, :, :], AX.X, ALU.max))
                    after(g, a)
                    V.tensor_tensor(kb[:, :, :], kb[:, :, :], kmax[:, :].unsqueeze(2).to_broadcast([128, R * H, K]),
                                    ALU.subtract).then_inc(sc_ready, 1)

                def softmax_end(g):
                    dve.wait_ge(sc_exp, g + 1)
                    a = done(V.tensor_reduce(ksum[:, :], kb[:, :, :], AX.X, ALU.add))
                    after(g, a)
                    a = done(V.reciprocal(krec[:, :], ksum[:, :]))
                    after(g, a)
                    V.tensor_tensor(kb[:, :, :], kb[:, :, :], krec[:, :].unsqueeze(2).to_broadcast([128, R * H, K]),
                                    ALU.mult).then_inc(weights_done, 1)
                    dve.wait_ge(weights_done, g + 1)

                def window(g, s):
                    lo, hi = SLICES[s]
                    acc = hg[:, lo:hi, :].rearrange("p a d -> p (a d)")
                    made, added = {}, {}

                    def mult(k):
                        if k >= 2:
                            after(g, added[k - 2])
                        made[k] = done(V.tensor_tensor(
                            prod[k % 2][:, 0:(hi - lo) * D].rearrange("p (a d) -> p a d", d=IPG),
                            vx[:, (lo + k) * D:(hi + k) * D].rearrange("p (a d) -> p a d", d=IPG),
                            kb[:, lo * H:hi * H, k:k + 1].to_broadcast([128, (hi - lo) * H, IPG]), ALU.mult))

                    def add(k):
                        after(g, max(made[k], added.get(k - 1, 0)))
                        added[k] = done(V.tensor_tensor(acc, acc, prod[k % 2][:, 0:(hi - lo) * D], ALU.add))
                    mult(0)
                    yield
                    for k in range(1, K):
                        mult(k)
                        yield
                        if s == 0 and k == 1:
                            dve.wait_ge(hg_loaded, 16 * GIMG * (g + 1))
                        add(k - 1)
                        yield
                    add(K - 1)
                    after(g, added[K - 1])
                    yield

                def slice_stats(g, s):
                    if s == NSL - 1:
                        dve.wait_ge(pool_sum, 2 * K * (g + 1))
                    settled(dve)
                    for r in range(*SLICES[s]):
                        ins = V.bn_stats(stats2[:, r, :], hg[:, r, :])
                        if r == SLICES[s][0]:
                            ins.then_inc(window_done, 1)
                    a = done(ins)
                    after(g, a)
                    settled(dve)
                    for r in range(*SLICES[s]):
                        ins = V.bn_aggr(mv2[:, r, :], stats2[:, r, :])
                    ins.then_inc(aggr2_done, 1)

                def top_two(g):
                    dve.wait_ge(lg_ready, g + 1)
                    a = done(V.tensor_copy(lg[:, :, :], bankN[:, 0:R * E].rearrange("p (r e) -> p r e", e=E)))
                    revv = rev[:, :].rearrange("p (r e) -> p r e", e=E)
                    src = lg
                    for k in range(TOPK):
                        after(g, a)
                        ins = V.tensor_reduce(m12[:, k, :], src[:, :, :], AX.X, ALU.max)
                        a = done(ins)
                        after(g, a)
                        if k == 0:
                            dve.sem_inc(lg_read, 1)
                        a = done(V.tensor_tensor(eq[:, :, :], src[:, :, :],
                                                 m12[:, k, :].unsqueeze(2).to_broadcast([128, R, E]), ALU.is_equal))
                        after(g, a)
                        a = done(V.tensor_tensor(eq[:, :, :], eq[:, :, :], revv, ALU.mult))
                        after(g, a)
                        a = done(V.tensor_reduce(i12[:, k, :], eq[:, :, :], AX.X, ALU.max))
                        after(g, a)
                        ohk = oh[:, k * E:(k + 1) * E, :].rearrange("p e r -> p r e")
                        a = done(V.tensor_tensor(ohk, revv, i12[:, k, :].unsqueeze(2).to_broadcast([128, R, E]),
                                                 ALU.is_equal))
                        if k == 0:
                            after(g, a)
                            a = done(V.scalar_tensor_tensor(lg2[:, :, :], ohk, -BIG, lg[:, :, :], ALU.mult, ALU.add))
                            src = lg2
                    V.tensor_tensor(gap[:, :], m12[:, 1, :], m12[:, 0, :], ALU.subtract).then_inc(gap_ready, 1)
                    after(g, a)
                    a = done(V.tensor_tensor(ohv[:, :, :], oh[:, :, :],
                                             val[:, :].unsqueeze(1).to_broadcast([128, TOPK * E, R]), ALU.mult))
                    after(g, a)
                    V.tensor_reduce(cnt[:, :], ohv[:, :, :], AX.X, ALU.add).then_inc(cnt_ready, 1)
                    a = done(V.tensor_tensor_scan(inc[:, :], ones[:, :], ohv[:, :, :].rearrange("p a r -> p (a r)"), 0.0,
                                                  ALU.mult, ALU.add))

                PLACES_STEPS = 16

                def places(g):
                    before = counted[0]
                    dve.wait_ge(ex_ready, g + 1)
                    b = done(V.tensor_scalar(gap[:, :], ex[:, :], 1.0, None, ALU.add))
                    after(g, b)
                    b = done(V.reciprocal(w12[:, 0, :], gap[:, :]))
                    after(g, b)
                    done(V.tensor_tensor(w12[:, 1, :], w12[:, 0, :], ex[:, :], ALU.mult))
                    dve.wait_ge(pre_ready, g + 1)
                    done(V.tensor_tensor(off[:, :], bankV[:, 0:16], base[:, :], ALU.add))
                    a = done(V.tensor_tensor(base[:, :], base[:, :], bankV[:, 16:32], ALU.add))
                    after(g, a)
                    ends = inc[:, :].rearrange("p (a r) -> p a r", r=R)[:, 0:TOPK * E - 1, R - 1]
                    ins = V.tensor_tensor(off[:, 1:16], off[:, 1:16], ends, ALU.subtract)
                    dve.sem_inc(pre_read, 1)
                    a = done(ins)
                    after(g, a)
                    a = done(V.tensor_tensor(pos[:, :, :], inc[:, :].rearrange("p (a r) -> p a r", r=R),
                                             off[:, :].unsqueeze(2).to_broadcast([128, 16, R]), ALU.add))
                    after(g, a)
                    done(V.tensor_tensor(pos[:, :, :], pos[:, :, :], ohv[:, :, :], ALU.mult))
                    a = done(V.tensor_tensor(pos2[:, :, :], ohv[:, :, :],
                                             sbase[:, :].unsqueeze(2).to_broadcast([128, 16, R]), ALU.mult))
                    after(g, a)
                    done(V.tensor_reduce(posk[:, :, :], pos[:, :, :].rearrange("p (k e) r -> p k r e", e=E), AX.X, ALU.add))
                    a = done(V.tensor_reduce(slotk[:, :, :], pos2[:, :, :].rearrange("p (k e) r -> p k r e", e=E), AX.X,
                                             ALU.add))
                    after(g, a)
                    done(V.tensor_scalar(keep[:, :, :], posk[:, :, :], float(CAP), None, ALU.is_le))
                    a = done(V.tensor_tensor(slotk[:, :, :], slotk[:, :, :], posk[:, :, :], ALU.add))
                    after(g, a)
                    a = done(V.tensor_tensor(keep[:, :, :], keep[:, :, :],
                                             val[:, :].unsqueeze(1).to_broadcast([128, TOPK, R]), ALU.mult))
                    after(g, a)
                    a = done(V.scalar_tensor_tensor(slotk[:, :, :], slotk[:, :, :], -float(NS), keep[:, :, :],
                                                    ALU.add, ALU.mult))
                    dve.wait_ge(rows_sent, g + 1)
                    V.tensor_copy(xrow[:, :, :].bitcast(fp32)[:, :, META // 2 + 1:META // 2 + 3],
                                  w12[:, :, :].rearrange("p k r -> p r k"))
                    V.tensor_copy(xrow[:, :, :].bitcast(i32)[:, :, META // 2:META // 2 + 1], tid[:, :].unsqueeze(2))
                    after(g, a)
                    V.tensor_scalar(idx[:, :, :], slotk[:, :, :], float(NS), None, ALU.add).then_inc(idx_ready, 1)
                    done(V.tensor_scalar(tid[:, :], tid[:, :], float(GIMG * L), None, ALU.add))
                    assert counted[0] == before + PLACES_STEPS

                dve.wait_ge(first_loaded, 16 * NFIRST)
                V.tensor_copy(idn16[:, :], idn[:, :])
                norm(0, 0, 0)
                dve.wait_ge(const_loaded, NCONST)
                for t in range(2):
                    for k in range(K):
                        last = V.tensor_scalar(conv_w[:, t, k, :], pw_sb[:, t, :], dw_sb[:, t, k:k + 1], None, ALU.mult)
                last.then_inc(conv_w_ready, 1)

                def body(it):
                    pairs, groups = not first(it, NIT - 1), not first(it)
                    g = it - 1
                    sums = [window(g, s) for s in range(NSL - 1)]

                    def part(s, n):
                        for _ in range(n):
                            next(sums[s])

                    beside = {
                        (0, 1): lambda: softmax_top(g),
                        (0, 2): lambda: softmax_end(g),
                        (0, 3): lambda: part(0, 7),
                        (1, 1): lambda: part(0, 6),
                        (1, 2): lambda: (part(0, 5), slice_stats(g, 0)),
                        (1, 3): lambda: part(1, 4),
                        (2, 1): lambda: part(1, 4),
                        (2, 2): lambda: part(1, 4),
                        (2, 3): lambda: part(1, 4),
                        (3, 0): lambda: (part(1, 2), slice_stats(g, 1), slice_stats(g, 2)),
                        (3, 3): lambda: top_two(g),
                    } if groups else {}
                    if groups and not first(it, 1):
                        places(g - 1)
                    if not pairs:
                        softmax_top(g)
                        softmax_end(g)
                        for k in range(K):
                            if k >= 2:
                                dve.wait_ge(tap_summed, k - 1)
                            n = SLICES[0][1]
                            V.tensor_tensor(prodL[k % 2].rearrange("p (a d) -> p a d", d=IPG),
                                            vx[:, k * D:(k + n) * D].rearrange("p (a d) -> p a d", d=IPG),
                                            kb[:, 0:n * H, k:k + 1].to_broadcast([128, n * H, IPG]), ALU.mult)\
                                .then_inc(tap_made, 1)
                            if k == 1:
                                dve.wait_ge(hg_loaded, 16 * GIMG * (g + 1))
                            part(1, 1)
                        part(1, 1)
                        dve.wait_ge(sum_out, 1)
                        slice_stats(g, 0)
                        part(1, 2 * K - 10)
                        slice_stats(g, 1)
                        slice_stats(g, 2)
                        top_two(g)
                        places(g)
                        return
                    for q in range(PPI):
                        p, j, u = PPI * it + q, 2 * it + q // 2, q % 2
                        for t in range(4):
                            if (q, t) in beside:
                                beside[q, t]()
                            if t < 3 and pairs:
                                attend(p, u, t)
                            if t == 0 and pairs and not last_pair(it, q):
                                norm(p + 1, j + u, 1 - u)
                    if groups and not per_group:
                        per_group.append(counted[0] + PLACES_STEPS)
                for it in range(2):
                    body(it)
                with dve.Fori(2, NIT - 2) as it:
                    body(it)
                body(NG - 1)
                body(NIT - 1)

            @block.tensor
            def _(pe):
                T_ = nc.tensor

                def patch(p, j, u):
                    pe.wait_ge(x_loaded[u], 16 * (j + 1))
                    for c in range(2):
                        wait(pe, h_in_rows, 2 * p + c - 1)
                        for m in range(2):
                            for kc in range(KC):
                                mm = T_.matmul(bankH[c][:, m * D:(m + 1) * D],
                                               xb[u][:, m, kc * TI + c * 128:kc * TI + c * 128 + 128],
                                               wp_sb[:, kc, :], start=(kc == 0), stop=(kc == KC - 1))
                        mm.then_inc(h_ready, 1)

                def transposes(p, u):
                    pe.wait_ge(qn_ready, p + 1)
                    for t in range(3):
                        wait(pe, qT_done, 3 * p + t - 1)
                        for c in range(3):
                            T = CT[c]
                            mm = T_.transpose(bankT[(u + t) % 2][:, c * 128:c * 128 + T],
                                              qn[u][0:T, c, TILE_AT[t]:TILE_AT[t] + 128], idn[0:T, 0:T])
                        mm.then_inc(tq_ready, 1)

                def conv(p, u, t, beside=None, at=()):
                    pe.wait_ge(qT_done, 3 * p + t + 1)
                    wait(pe, ca_done, 3 * p + t - 1)
                    for k in range(K):
                        mm = T_.matmul(bankK[(u + t) % 2][:, 0:L], conv_w[:, t // 2, k, :],
                                       qT[u][:, t, k:k + L], start=(k == 0), stop=(k == K - 1))
                        if k == K - 1:
                            mm.then_inc(key_ready, 1)
                        if k in at:
                            next(beside)

                def values(p, u, c):
                    pe.wait_ge(qT_done, 3 * p + 3)
                    wait(pe, v_evac, 3 * p + c)
                    T, lo = CT[c], PAD + 128 * c
                    T_.matmul(bankV[0:T, 0:D], qT[u][:, 0, lo:lo + T], ptA_sb[:, :], start=True, stop=False)
                    T_.matmul(bankV[0:T, D:2 * D], qT[u][:, 1, lo:lo + T], ptA_sb[:, :], start=False, stop=False)
                    T_.matmul(bankV[0:T, 0:2 * D], qT[u][:, 2, lo:lo + T], ptB_sb[:, :], start=False, stop=True)\
                      .then_inc(v_ready, 1)

                def scores(p, u, c):
                    pe.wait_ge(ca_done, 3 * p + 3)
                    wait(pe, kern_evac, 3 * p + c)
                    T, n = CT[c], HA * K
                    for t in range(3):
                        mm = T_.matmul(bankN[0:T, t * n:(t + 1) * n], ca[u][:, t, 128 * c:128 * c + T],
                                       (akB_sb if t == 2 else akA_sb)[:, :], start=True, stop=True)
                    mm.then_inc(kern_ready, 1)

                def logits(g, p):
                    pe.wait_ge(qT_done, 3 * p + 3)
                    pe.wait_ge(kern_evac, 3 * p)
                    for n, r in enumerate(PAIRS):
                        have = sum(r + 1 >= hi for _, hi in SLICES) + 1
                        pe.wait_ge(xn_ready, NSL * g + have)
                        if n > 1:
                            pe.wait_ge(tr_evac, NQ * g + n - 1)
                        for i in range(3):
                            mm = T_.transpose(bankT[n % 2][:, i * 128:(i + 1) * 128],
                                              hg[:, r:r + 2, :].rearrange("p r d -> p (r d)")[:, i * 128:(i + 1) * 128],
                                              idn[:, :])
                        mm.then_inc(tr_ready, 1)
                        if n:
                            route(g, n - 1)
                        yield
                    route(g, NQ - 1).then_inc(lg_ready, 1)
                    yield

                def route(g, n):
                    r = PAIRS[n]
                    pe.wait_ge(tr_evac, NQ * g + n + 1)
                    for i, w in ((0, wgA), (1, wgC)):
                        T_.matmul(bankN[:, (r + i) * E:(r + i + 1) * E], xTr[n % 2][:, i * 256:i * 256 + 128], w[:, :],
                                  start=(i == 0), stop=False)
                    mm = T_.matmul(bankN[:, r * E:(r + 2) * E], xTr[n % 2][:, 128:256], wgP[:, :], start=False, stop=True)
                    if n < NQ - 1:
                        mm.then_inc(routed, 1)
                    return mm

                def counts_before(g, p):
                    pe.wait_ge(cnt_ready, g + 1)
                    pe.wait_ge(v_evac, 3 * p)
                    T_.matmul(bankV[:, 0:16], low_sb[:, :], cnt[:, :], start=True, stop=True)
                    T_.matmul(bankV[:, 16:32], ones[:, 0:128], cnt[:, :], start=True, stop=True).then_inc(pre_ready, 1)

                ROUNDS = [(1, 3, 5, 7), (), (0, 1, 2, 3, 4, 5, 6, 7)]
                pe.wait_ge(first_loaded, 16 * NFIRST)
                pe.wait_ge(zeroed, 1)
                patch(0, 0, 0)
                transposes(0, 0)
                patch(1, 0, 1)

                def body(it):
                    pairs, groups = not first(it, NIT - 1), not first(it)
                    if not pairs:
                        counts_before(it - 2, NPAIR)
                        pe.wait_ge(hg_loaded, 16 * B)
                        pe.wait_ge(ca_done, 3 * NPAIR)
                        pe.wait_ge(h_in_rows, 2 * NPAIR)
                        for b, n in enumerate(LCOLS):
                            T_.matmul(bankL[b][:, 0:n], idn[:, :], hgf[:, b * 512:b * 512 + n], start=True, stop=False)
                        for k in range(K):
                            pe.wait_ge(tap_made, k + 1)
                            for b, n in enumerate(LCOLS):
                                mm = T_.matmul(bankL[b][:, 0:n], idn[:, :], prodL[k % 2][:, b * 512:b * 512 + n],
                                               start=False, stop=(k == K - 1))
                            mm.then_inc(tap_summed, 1)
                        for _ in logits(it - 1, NPAIR - 1):
                            pass
                        counts_before(it - 1, NPAIR)
                        return
                    for q in range(PPI):
                        p, j, u = PPI * it + q, 2 * it + q // 2, q % 2
                        routing = q == 3 and groups
                        if first(it) and q == 0:
                            pe.wait_ge(const_loaded, NCONST)
                            pe.wait_ge(conv_w_ready, 1)
                        router = logits(it - 1, p) if routing else None

                        def more_patches():
                            if not (first(it, NG - 1) and q >= 2):
                                patch(p + 2, j + 1, u)
                        if q == 0 and groups and not first(it, 1):
                            counts_before(it - 2, p)
                        for t in range(3):
                            if routing and t == 2:
                                more_patches()
                            conv(p, u, t, router, ROUNDS[t] if routing else ())
                            if q == 0 and t == 0 and groups and not first(it, 1):
                                pe.wait_ge(pre_read, it - 1)
                            values(p, u, t)
                        if not last_pair(it, q):
                            transposes(p + 1, 1 - u)
                        if not routing:
                            more_patches()
                        if routing:
                            pe.wait_ge(lg_read, it)
                        for c in range(3):
                            scores(p, u, c)
                for it in range(2):
                    body(it)
                with pe.Fori(2, NIT - 2) as it:
                    body(it)
                body(NG - 1)
                body(NIT - 1)

        st = ExitStack()
        with st:
            sb, pb, sem = allocator(st)
            NJ, NCH = HID // 128, SLOT_TILE // CHUNK
            NG2 = -(-NCH // 2)
            F1 = 2 * HID
            wstage = sb("wstage", [128, 2 * F1 + NJ * D])
            wh = [sb(f"w_high{n}", [128, 2 * F1 + NJ * D], fp16) for n in range(2)]
            wl = [sb(f"w_low{n}", [128, 2 * F1 + NJ * D], fp16) for n in range(2)]
            NMETA = 5
            xin = [sb(f"xin{n}", [CHUNK, NCH, XW], u16) for n in range(2)]
            meta = [sb(f"meta{n}", [CHUNK, NCH, 4], i32) for n in range(NMETA)]
            wsl = [sb(f"slot_weight{n}", [CHUNK, NCH]) for n in range(NMETA)]
            xT = [sb(f"xeT{n}", [128, 3 * SLOT_TILE], fp16) for n in range(2)]
            sg = [sb(f"silu{n}", [128, HALF]) for n in range(2)]
            hf = [sb(f"hidden32_{n}", [128, SLOT_TILE]) for n in range(2)]
            hh = [sb(f"hidden_high{n}", [128, NJ, SLOT_TILE], fp16) for n in range(2)]
            hl = [sb(f"hidden_low{n}", [128, NJ, SLOT_TILE], fp16) for n in range(2)]
            yb = [sb(f"yb{n}", [CHUNK, NCH, D]) for n in range(2)]
            BX = 1024
            bankX = [pb("bankX0", fp16), pb("bankX1", fp16)]
            bankU = [pb(f"bankU{n}") for n in range(2)]
            bankG = [pb(f"bankG{n}") for n in range(2)]
            bankY = [pb(f"bankY{n}") for n in range(2)]

            w_loaded, w_high, w_low = sem("w_loaded"), sem("w_high_done"), sem("w_low_done")
            xin_loaded = [sem(f"xin_loaded{n}") for n in range(2)]
            added = [sem(f"added{n}") for n in range(2)]
            meta_done = sem("meta_done")
            xt_ready, x0_evac, x1_evac = sem("xt_ready"), sem("x0_evac"), sem("x1_evac")
            up_ready, gate_ready = sem("up_ready"), sem("gate_ready")
            silu_done, prod_done, hi_done, lo_done = sem("silu_done"), sem("prod_done"), sem("hi_done"), sem("lo_done")
            y_ready, y_evac = sem("y_ready"), sem("y_evac")
            last_sent = [sem(f"last_sent{k}") for k in range(TOPK)]
            block = st.enter_context(nc.Block())
            BODY = 2 * TPE
            NT = E * TPE
            NU = 2 * NJ
            LASTB = E // 2 - 1

            def is_last(i):
                return isinstance(i, int) and i == LASTB

            def loop(eng, body):
                body(0)
                with eng.Fori(1, LASTB) as i:
                    body(i)
                body(LASTB)

            def adds(v, i, t):
                return 16 * NCH * (BODY // 2 * i + (t + 1 - v) // 2)

            @block.sync
            def _(sp):
                def load_w(e):
                    for dst, src in ((wstage[:, 0:F1], W1[bass.ds(e, 1), 0:128, :].rearrange("e p f -> p (e f)")),
                                     (wstage[0:D2, F1:2 * F1], W1[bass.ds(e, 1), 128:D, :].rearrange("e p f -> p (e f)")),
                                     (wstage[D2:128, F1:2 * F1], W1[bass.ds(e, 1), 128:D, :].rearrange("e p f -> p (e f)")),
                                     (wstage[:, 2 * F1:].rearrange("p (j d) -> p j d", d=D),
                                      W2[bass.ds(e, 1), :, :].rearrange("e (j p) d -> p (e j) d", p=128))):
                        sp.dma_start(dst, src).then_inc(w_loaded, 16)

                def body(i):
                    for t in range(BODY):
                        n, ee = BODY * i + t, t // TPE
                        wait(sp, xt_ready, n - 1)
                        wait(sp, meta_done, n - 1)
                        if isinstance(i, int) and i == 0 and t in (0, MIX):
                            sp.wait_ge(last_sent[t // MIX], 16 * R)
                        sp.dma_start(xin[t % 2][:, :, :], xslots[bass.ds(n * SLOT_TILE, SLOT_TILE), :]
                                     .rearrange("(p j) f -> p j f", j=NCH)).then_inc(xin_loaded[t % 2], 16)
                        if t % TPE == 1 and not (is_last(i) and ee == 1):
                            e = 2 * i + ee + 1
                            wait(sp, w_high, e)
                            wait(sp, w_low, e)
                            load_w(e)
                load_w(0)
                loop(sp, body)

            @block.gpsimd
            def _(pool):
                for n in range(TOPK * R):
                    scatter_rows(n, last_sent[n // R])

                def body(i):
                    for t in range(BODY):
                        n, v = BODY * i + t, t % 2
                        pool.wait_ge(y_evac, NG2 * (n + 1))
                        if t % TPE == 0:
                            for v2 in range(2):
                                wait(pool, added[v2], adds(v2, i, t))
                        settled(pool)
                        for c in range(NCH):
                            nc.gpsimd.indirect_dma_start(
                                out=out[:, :], out_offset=bass.IndirectOffsetOnAxis(ap=meta[t % NMETA][:, c, 0:1], axis=0),
                                in_=yb[v][:, c, :], in_offset=None, compute_op=ALU.add).then_inc(added[v], 16)
                loop(pool, body)
                for v in range(2):
                    pool.wait_ge(added[v], adds(v, E // 2, 0))

            @block.scalar
            def _(act):
                def split_w(e, ee):
                    act.wait_ge(w_loaded, 64 * (e + 1))
                    nc.scalar.mul(wh[ee][:, :], wstage[:, :], WSCALE).then_inc(w_high, 1)

                def inputs_out(i, t):
                    n, v = BODY * i + t, t % 2
                    act.wait_ge(xt_ready, n + 1)
                    wait(act, up_ready, NU * (n - 1))
                    nc.scalar.copy(xT[v][:, 0:BX], bankX[0][:, :]).then_inc(x0_evac, 1)
                split_w(0, 0)
                inputs_out(0, 0)

                def body(i):
                    for t in range(BODY):
                        n, v, ee = BODY * i + t, t % 2, t // TPE

                        def high(j):
                            act.wait_ge(prod_done, NU * n + 2 * j + 2)
                            if j == 0:
                                wait(act, y_ready, NG2 * (n - 1))
                            nc.scalar.copy(hh[v][:, j, :], hf[j % 2][:, :]).then_inc(hi_done, 1)
                        for j in range(NJ):
                            for m in range(2):
                                w = 2 * j + m
                                act.wait_ge(gate_ready, NU * n + w + 1)
                                wait(act, prod_done, NU * n + w - 1)
                                nc.scalar.activation(sg[m][:, :], bankG[m][:, 0:HALF], ACT.Silu,
                                                     scale=1 / WSCALE).then_inc(silu_done, 1)
                            if j:
                                high(j - 1)
                            if j == 2 and t + 1 < BODY:
                                inputs_out(i, t + 1)
                        high(NJ - 1)
                        if t + 1 == BODY and not is_last(i):
                            inputs_out(i + 1, 0)
                        if t % TPE == 2 and not (is_last(i) and ee == 1):
                            wait(act, y_ready, NG2 * (n - 2))
                            split_w(2 * i + ee + 1, 1 - ee)
                loop(act, body)

            @block.vector
            def _(dve):
                V = nc.vector

                def split_w(e, ee):
                    dve.wait_ge(w_high, e + 1)
                    V.scalar_tensor_tensor(wl[ee][:, :], wstage[:, :], WSCALE, wh[ee][:, :], ALU.mult, ALU.subtract)\
                        .then_inc(w_low, 1)

                def inputs_out(i, t):
                    n, v = BODY * i + t, t % 2
                    dve.wait_ge(xt_ready, n + 1)
                    wait(dve, up_ready, NU * (n - 1))
                    V.tensor_copy(xT[v][:, BX:3 * SLOT_TILE], bankX[1][:, 0:3 * SLOT_TILE - BX]).then_inc(x1_evac, 1)
                split_w(0, 0)
                inputs_out(0, 0)

                def evac_y(i, t, first_t):
                    n, v = BODY * i + t, t % 2
                    wait(dve, added[v], adds(v, i, t))
                    for b in range(NG2):
                        dve.wait_ge(y_ready, NG2 * n + b + 1)
                        for c in range(2 * b, min(2 * b + 2, NCH)):
                            last = V.tensor_scalar(yb[v][:, c, :], bankY[(NG2 * t + b) % 2][:, (c % 2) * D:(c % 2 + 1) * D],
                                                   wsl[t % NMETA][:, c:c + 1], None, ALU.mult)
                        last.then_inc(y_evac, 1)

                def body(i):
                    for t in range(BODY):
                        n, v, ee, te = BODY * i + t, t % 2, t // TPE, t % TPE
                        dve.wait_ge(xin_loaded[v], 16 * (BODY // 2 * i + t // 2 + 1))
                        wait(dve, added[(t - NMETA) % 2], adds((t - NMETA) % 2, i, t - NMETA + 1))
                        xm = xin[v][:, :, :].bitcast(i32)
                        V.tensor_copy(meta[t % NMETA][:, :, :], xm[:, :, META // 2:META // 2 + 4])
                        parts = [(0, CHUNK, int(te > MIX))] if te != MIX else [(0, MIXP, 0), (MIXP, CHUNK, 1)]
                        for lo, hi, k in parts:
                            last = V.tensor_scalar(wsl[t % NMETA][lo:hi, :],
                                                   xin[v][lo:hi, :, :].bitcast(fp32)[:, :, META // 2 + 1 + k],
                                                   WSCALE ** -2, None, ALU.mult)
                        last.then_inc(meta_done, 1)

                        def low(j):
                            dve.wait_ge(hi_done, NJ * n + j + 1)
                            V.tensor_tensor(hl[v][:, j, :], hf[j % 2][:, :], hh[v][:, j, :], ALU.subtract)\
                                .then_inc(lo_done, 1)
                        for j in range(NJ):
                            for m in range(2):
                                w = 2 * j + m
                                dve.wait_ge(silu_done, NU * n + w + 1)
                                dve.wait_ge(up_ready, NU * n + w + 1)
                                if m == 0:
                                    wait(dve, lo_done, NJ * n + j - 1)
                                V.tensor_tensor(hf[j % 2][:, m * HALF:(m + 1) * HALF], sg[m][:, :],
                                                bankU[m][:, 0:HALF], ALU.mult).then_inc(prod_done, 1)
                            if j:
                                low(j - 1)
                            if j == 2 and t + 1 < BODY:
                                inputs_out(i, t + 1)
                        low(NJ - 1)
                        if t + 1 == BODY and not is_last(i):
                            inputs_out(i + 1, 0)
                        if t:
                            evac_y(i, t - 1, t)
                        if t % TPE == 2 and not (is_last(i) and ee == 1):
                            split_w(2 * i + ee + 1, 1 - ee)
                    evac_y(i, BODY - 1, BODY)
                loop(dve, body)

            @block.tensor
            def _(pe):
                T_ = nc.tensor

                def tr(i, t):
                    n, v = BODY * i + t, t % 2
                    pe.wait_ge(xin_loaded[v], 16 * (BODY // 2 * i + t // 2 + 1))
                    wait(pe, x0_evac, n)
                    wait(pe, x1_evac, n)
                    for c in range(NCH):
                        for at, ch in ((0, 0), (SLOT_TILE, 128), (2 * SLOT_TILE, LOA)):
                            b, col = divmod(at + c * CHUNK, BX)
                            mm = T_.transpose(bankX[b][:, col:col + CHUNK], xin[v][:, c, ch:ch + 128].bitcast(fp16),
                                              idn16[:, :])
                    mm.then_inc(xt_ready, 1)

                def up(i, t):
                    n, v, ee = BODY * i + t, t % 2, t // TPE
                    if t % TPE == 0:
                        pe.wait_ge(w_high, 2 * i + ee + 1)
                        pe.wait_ge(w_low, 2 * i + ee + 1)
                    pe.wait_ge(x0_evac, n + 1)
                    pe.wait_ge(x1_evac, n + 1)
                    for j in range(NJ):
                        for m in range(2):
                            high, both, low = (xT[v][:, q * SLOT_TILE + m * HALF:q * SLOT_TILE + (m + 1) * HALF] for q in range(3))
                            for half, bank, ready, free in ((1, bankG, gate_ready, silu_done), (0, bankU, up_ready, prod_done)):
                                wait(pe, free, NU * n + 2 * j + m - 1)
                                lo = half * HID + j * 128
                                o = bank[m][:, 0:HALF]
                                T_.matmul(o, wh[ee][:, lo:lo + 128], high, start=True, stop=False)
                                T_.matmul(o, wh[ee][:, lo:lo + 128], low, start=False, stop=False)
                                T_.matmul(o, wl[ee][:, lo:lo + 128], high, start=False, stop=False)
                                T_.matmul(o, wh[ee][:, F1 + lo:F1 + lo + 128], both, start=False, stop=False)
                                T_.matmul(o, wl[ee][:, F1 + lo:F1 + lo + 128], both, start=False, stop=True)\
                                  .then_inc(ready, 1)

                def down(i, t):
                    n, v, ee = BODY * i + t, t % 2, t // TPE
                    pe.wait_ge(lo_done, NJ * n + NJ)
                    for b in range(NG2):
                        wait(pe, y_evac, NG2 * n + b - 1)
                        for c in range(2 * b, min(2 * b + 2, NCH)):
                            cs = slice(c * CHUNK, (c + 1) * CHUNK)
                            o = bankY[(NG2 * t + b) % 2][:, (c % 2) * D:(c % 2 + 1) * D]
                            for j in range(NJ):
                                ws = slice(2 * F1 + j * D, 2 * F1 + (j + 1) * D)
                                T_.matmul(o, hh[v][:, j, cs], wh[ee][:, ws], start=(j == 0), stop=False)
                                T_.matmul(o, hh[v][:, j, cs], wl[ee][:, ws], start=False, stop=False)
                                mm = T_.matmul(o, hl[v][:, j, cs], wh[ee][:, ws], start=False, stop=(j == NJ - 1))
                        mm.then_inc(y_ready, 1)

                tr(0, 0)

                def body(i):
                    for t in range(BODY):
                        if t + 1 < BODY:
                            tr(i, t + 1)
                        elif not is_last(i):
                            tr(i + 1, 0)
                        up(i, t)
                        if t:
                            down(i, t - 1)
                    down(i, BODY - 1)
                loop(pe, body)


def _hilbert():
    pts = []
    for d in range(TI):
        t, x, y, s = d, 0, 0, 1
        while s < CURVE:
            rx = 1 & t // 2
            ry = 1 & (t ^ rx)
            if ry == 0:
                if rx == 1:
                    x, y = s - 1 - x, s - 1 - y
                x, y = y, x
            x, y, t, s = x + s * rx, y + s * ry, t // 4, s * 2
        pts.append((min(x, GRID - 1), min(y, GRID - 1)))
    return np.array(pts)


def _layout(a):
    f = np.float32
    pts = _hilbert()
    xs = np.asarray(a["x"]).reshape(B, CIN, GRID, PATCH, GRID, PATCH)
    xs = xs[:, :, pts[:, 0], :, pts[:, 1], :]
    xs = xs.transpose(1, 2, 3, 4, 0).reshape(B, KC, 128, TI).transpose(0, 2, 1, 3).reshape(B, 128, KC * TI)
    wt = np.asarray(a["L0_tok_W"]).reshape(D, KC, 128).transpose(2, 1, 0)
    dwt = np.asarray(a["L0_attn_dw_w"]).reshape(D, K)
    dwl = np.stack([dwt[:128], np.concatenate([dwt[128:], dwt[128:]])], 1)
    pww, akw = np.asarray(a["L0_attn_pw_w"]), np.asarray(a["L0_attn_ak_w"])
    heads = [list(range(HA)), list(range(HA, H)) * 2]
    pwl = np.zeros((128, 2, 128), f)
    akl = [np.zeros((128, HA * K), f), np.zeros((128, HA * K), f)]
    for t in range(2):
        for n, h in enumerate(heads[t]):
            pwl[n * IPG:(n + 1) * IPG, t, n * IPG:(n + 1) * IPG] = pww[h].T
            akl[t][n * IPG:(n + 1) * IPG, n * K:(n + 1) * K] = akw[h].T
    pb = np.asarray(a["L0_attn_pw_b"])
    pwbl = np.stack([pb[:128], np.concatenate([pb[128:], pb[128:]])], 1)
    ptt = np.asarray(a["L0_attn_pt_w"]).T
    ptBl = np.zeros((128, 2 * D), f)
    ptBl[:D2, :D] = ptt[128:]
    ptBl[D2:, D:] = ptt[128:]

    def rep(v, n=1):
        return np.broadcast_to(np.tile(np.asarray(v), n), (128, n * len(v)))
    wgate = np.asarray(a["L0_ffn_Wg"])
    wgpair = np.zeros((128, 2 * E), f)
    wgpair[:D2, :E] = wgate[128:]
    wgpair[D2:, E:] = wgate[:D2]
    revrank = np.broadcast_to(np.tile(E - np.arange(E), R), (128, R * E)).astype(f)
    valid = np.array([[(p % SEG) * R + r < L for r in range(R)] for p in range(128)]).astype(f)
    tokid = np.array([[(p // SEG) * L + (p % SEG) * R + r for r in range(R)] for p in range(128)]).astype(f)
    slotbase = np.broadcast_to(np.array([e * CAPE + k * CAPK - 1 for k in range(TOPK) for e in range(E)]), (128, 16))
    return {
        "x": xs, "txt": np.asarray(a["txt"]), "wpatch": wt, "tokb": rep(a["L0_tok_b"], 2), "dw": dwl, "pw": pwl,
        "pwb": pwbl, "akA": akl[0], "akB": akl[1], "akb": rep(a["L0_attn_ak_b"]), "ptA": ptt[:128], "ptB": ptBl,
        "ptb": rep(a["L0_attn_pt_b"], 2), "wg": wgate, "wgpair": wgpair, "W1": np.asarray(a["L0_ffn_W1"]),
        "W2": np.asarray(a["L0_ffn_W2"]), "ident": np.eye(128, dtype=f),
        "lower": np.triu(np.ones((128, 128), f), 1), "revrank": revrank, "valid": valid,
        "slotbase": slotbase.astype(f), "tokid": tokid,
    }


def kernel(**inputs):
    import concourse.bacc as _bacc
    from concourse.bass_utils import run_bass_kernel_spmd as _run

    nc = _bacc.Bacc("TRN2", target_bir_lowering=False, num_devices=1)
    arrays, args = {}, {}
    for name, a in _layout(inputs).items():
        a = np.ascontiguousarray(a)
        arrays[f"in_{name}"] = a
        args[name] = nc.dram_tensor(f"in_{name}", a.shape, mybir.dt.from_np(a.dtype), kind="ExternalInput").ap()
    args["out"] = nc.dram_tensor("out_0", (N + 2 * SLOT_TILE, D), mybir.dt.float32, kind="ExternalOutput").ap()
    build(nc, **args)
    r = _run(nc, [arrays], core_ids=[0])
    return r.results[0]["out_0"][:N].reshape(B, L, D)
```
